# Optimizing a Trainium2 kernel written in Bass

```python
import numpy as np
import jax
import jax.numpy as jnp

def _softmax(x, axis=-1):
    return jax.nn.softmax(x, axis=axis)
def _gelu(x):
    return jax.nn.gelu(x, approximate=True)
def _silu(x):
    return jax.nn.silu(x)
def _sigmoid(x):
    return jax.nn.sigmoid(x)
def _layernorm(x, axis=-1, eps=1e-5):
    m = jnp.mean(x, axis=axis, keepdims=True)
    v = jnp.var(x, axis=axis, keepdims=True)
    return (x - m) / jnp.sqrt(v + eps)
def _scatter_add(tgt, idx, src, axis=0):
    return tgt.at[idx].add(src)
def _segment_sum(src, seg, n):
    return jax.ops.segment_sum(src, seg, n)

kernel_name = 'mk_conv_preact_d2_conv_nchw128_67c502'

def setup_inputs(seed: int = 0):
    np.random.seed(seed)
    _w = jnp.asarray
    def _rec_inputs():
        import jax
        import jax.numpy as jnp
        _gk = jax.random.key(seed)
        x = -0.000125 + 0.9999 * jax.random.normal(jax.random.fold_in(_gk, 1), (16, 128, 128, 128), jnp.float32)
        return x
    x = _rec_inputs()
    def _L0_conv_setup():
        import jax, jax.numpy as jnp
        import numpy as np
        key = jax.random.key(seed)
        k1, k2 = jax.random.split(key)
        x = jax.random.normal(k1, (16, 128, 128, 128), dtype=jnp.float32)
        weight = jax.random.normal(k2, (128, 128, 3, 3), dtype=jnp.float32)
        return {'x': x, 'weight': weight}
    _L0_conv_all = _L0_conv_setup()
    _L0_conv_in = {k: v for k, v in _L0_conv_all.items() if k in ('weight', )}
    del _L0_conv_all

    def _L1_conv_setup():
        import jax, jax.numpy as jnp
        import numpy as np
        key = jax.random.key(seed)
        k1, k2 = jax.random.split(key)
        z_e = jax.random.normal(k1, (32, 128, 64, 64), dtype=jnp.float32)
        embedding = jax.random.normal(k2, (512, 128), dtype=jnp.float32)
        return {'z_e': z_e, 'embedding': embedding}
    _L1_conv_all = _L1_conv_setup()
    _L1_conv_in = {k: v for k, v in _L1_conv_all.items() if k in ('embedding', )}
    del _L1_conv_all

    return {
        "x": x,
        "L0_conv_weight": _L0_conv_in["weight"],
        "L1_conv_embedding": _L1_conv_in["embedding"],
    }

def reference(x, L0_conv_weight, L1_conv_embedding):
    import jax
    import jax.numpy as jnp
    def _L0_conv_ref(x, weight):
        import jax, jax.numpy as jnp
        import numpy as np
        B, C, H, W = x.shape
        out_ch, in_ch, k, _ = weight.shape
        weight_padded = jnp.pad(weight, ((0, 0), (0, 0), (0, H - k), (0, W - k)))
        X_f = jnp.fft.rfft2(x)
        W_f = jnp.fft.rfft2(weight_padded)
        Y_f = jnp.einsum('bchw,ochw->bohw', X_f, W_f)
        y = jnp.fft.irfft2(Y_f, s=(H, W))
        return y

    def _L1_conv_ref(z_e, embedding):
        import jax, jax.numpy as jnp
        import numpy as np
        B, C, H, W = z_e.shape
        z_flat = jnp.transpose(z_e, (0, 2, 3, 1)).reshape(-1, C)
        dist = jnp.sum(z_flat * z_flat, axis=1, keepdims=True) + jnp.sum(embedding * embedding, axis=1)[None, :] - 2.0 * jnp.einsum('nc,kc->nk', z_flat, embedding)
        indices = jnp.argmin(dist, axis=1)
        z_q = embedding[indices].reshape(B, H, W, C)
        return jnp.transpose(z_q, (0, 3, 1, 2))

    def _gn(v, G=32, eps=1e-5):
        B_, C_, H_, W_ = v.shape
        g = v.reshape(B_, G, C_ // G, H_, W_)
        m = jnp.mean(g, axis=(2, 3, 4), keepdims=True)
        s = jnp.var(g, axis=(2, 3, 4), keepdims=True)
        return ((g - m) / jnp.sqrt(s + eps)).reshape(v.shape)

    def _ln_c(v, eps=1e-6):
        m = jnp.mean(v, axis=1, keepdims=True)
        s = jnp.var(v, axis=1, keepdims=True)
        return (v - m) / jnp.sqrt(s + eps)

    def _ln_t(v, eps=1e-5):
        m = jnp.mean(v, axis=-1, keepdims=True)
        s = jnp.var(v, axis=-1, keepdims=True)
        return (v - m) / jnp.sqrt(s + eps)

    def _to_tokens(v):
        B_, C_, H_, W_ = v.shape
        return v.reshape(B_, C_, H_ * W_).transpose(0, 2, 1)
    def _from_tokens(t, like):
        B_, C_, H_, W_ = like.shape
        return t.transpose(0, 2, 1).reshape(B_, C_, H_, W_)

    x = x + _L0_conv_ref(_gn(x), L0_conv_weight)
    x = x + _L1_conv_ref(_gn(x), L1_conv_embedding)
    return x


_drawn_inputs = setup_inputs


def setup_inputs(seed=0):
    import zlib

    import numpy as np

    out = dict(_drawn_inputs(seed))
    spreads = {}
    factors = {}
    for name, (base, spread) in spreads.items():
        noise = np.random.default_rng([zlib.crc32(name.encode()), seed]).standard_normal(out[name].shape)
        drawn = base * np.exp(spread * noise) if base else spread * noise
        out[name] = jnp.asarray(drawn.astype(out[name].dtype))
    for name, factor in factors.items():
        out[name] = (out[name] * factor).astype(out[name].dtype)
    return out
```

```python
from contextlib import ExitStack

import numpy as np

import concourse.bass as bass
from concourse import mybir

F32 = mybir.dt.float32
F16 = mybir.dt.float16
I32 = mybir.dt.int32
U32 = mybir.dt.uint32
ALU = mybir.AluOpType
ACT = mybir.ActivationFunctionType
AX = mybir.AxisListType

P = 128
IMGS, H, W = 16, 128, 128
CODES = 512
BLOCKS = CODES // P
TAPS = 9
ROWS = 4
CH = ROWS * W
TILES = CH // P
CPI = H // ROWS
PPI = CPI // 2
PAIRS = IMGS * PPI
HALO = 2
GROUP = 4
EPS = 1e-5

L_STAT = PPI + 1
L_LOAD = L_STAT + 2
L_VQZ = PPI + 1
L_VQ = L_VQZ + 1
RING = L_LOAD + L_VQ + 3

ZS = 128.0
WS = 256.0

C_ID, C_GRP, C_CODE = 0, P, 2 * P
C_ALL = 2 * P + BLOCKS


def constants():
    c = np.zeros((P, C_ALL), np.float32)
    c[:, C_ID:C_ID + P] = np.eye(P)
    c[:, C_GRP:C_GRP + P] = np.kron(np.eye(P // GROUP), np.full((GROUP, GROUP), 1.0 / GROUP))
    c[:, C_CODE:C_CODE + BLOCKS] = np.arange(P)[:, None] + P * np.arange(BLOCKS)[None, :]
    return c


def walk(eng, pair, gn):
    def span(lo, hi, on):
        with eng.Fori(lo, hi) as t:
            pair(t, on)

    front = {"stats1"}
    conv = {"stats1", "convz", "conv", "evac0", "evac1"}
    full = conv | {"vqz", "vq", "out0", "out1", "reuse"}
    with eng.Fori(0, L_STAT - 1) as i:
        pair(i - L_STAT, front)
    gn(1, 0)
    pair(-1, {"stats1", "convz"}, first=True)
    pair(0, conv - {"evac0"})
    pair(1, conv)
    span(2, 15, conv)
    gn(1, 1)
    pair(15, conv, first=True)
    pair(16, conv, mid=0)
    pair(17, conv | {"vqz"})
    pair(18, conv | {"vqz", "vq", "out1"})
    for t in range(19, 21):
        pair(t, full - {"reuse"})
    span(21, 31, full)
    with eng.Fori(1, IMGS - 2) as j:
        gn(1, j + 1)
        pair(PPI * j + 15, full, first=True)
        pair(PPI * j + 16, full, mid=j)
        with eng.Fori(PPI * j + 17, PPI * j + 31) as t:
            pair(t, full)
    late = full - {"stats1"}
    j = IMGS - 2
    gn(1, j + 1)
    pair(PPI * j + 15, late, first=True)
    pair(PPI * j + 16, late, mid=j)
    span(PPI * j + 17, PPI * j + 31, late)
    pair(PAIRS - 1, late - {"convz"})
    tail = {"vqz", "vq", "out0", "out1"}
    pair(PAIRS, tail | {"evac0"}, mid=IMGS - 1)
    span(PAIRS + 1, PAIRS + L_VQZ, tail)
    pair(PAIRS + L_VQZ, tail - {"vqz"})
    pair(PAIRS + L_VQ, {"out0"})


def program(nc, x, weight, embedding, const, out):
    ctx = ExitStack()
    with ctx:
        def sb(name, shape, dt=F32):
            return ctx.enter_context(nc.sbuf_tensor(name, shape, dt))

        def pb(name, shape, dt=F32):
            return ctx.enter_context(nc.psum_tensor(name, shape, dt))

        def sem(name):
            return ctx.enter_context(nc.semaphore(name))

        ring = sb("ring", [P, RING, 2, CH])
        cst = sb("cst", [P, C_ALL])
        id16 = sb("id16", [P, P], F16)
        wT = sb("wT", [P, 2, TAPS, P], F16)
        eT = sb("eT", [P, 2, CODES], F16)
        eR = sb("eR", [P, 2, BLOCKS, P], F16)
        code_bias = sb("code_bias", [P, CODES])
        z32c = [sb(f"z32c{h}", [P, CH]) for h in range(2)]
        zc = [sb(f"zc{h}", [P, 2, ROWS + HALO, W + HALO], F16) for h in range(2)]
        z32v = [sb(f"z32v{h}", [P, CH]) for h in range(2)]
        zv = [sb(f"zv{h}", [P, 2, CH], F16) for h in range(2)]
        scores = [sb(f"scores{k}", [P, CODES]) for k in range(2)]
        best = [sb(f"best{k}", [P, 8]) for k in range(2)]
        place = [sb(f"place{h}", [P, TILES, 8], U32) for h in range(2)]
        idx16 = [sb(f"idx16{h}", [P, TILES], F16) for h in range(2)]
        idx_row = [sb(f"idx_row{h}", [P, CH], F16) for h in range(2)]
        onehot = [sb(f"onehot{h}", [P, BLOCKS, CH], F16) for h in range(2)]
        stat = [None, sb("stat1", [P, CPI, 6]), sb("stat2", [P, CPI, 6])]
        gn_ab = [None, sb("gn_ab1", [P, 2]), sb("gn_ab2", [P, 2])]
        gt = sb("gt", [P, 16])
        small = sb("small", [P, 16])
        conv_scale = small[:, 0:1]
        code_scale = small[:, 1:2]

        def scratch(slot, shape):
            n = int(np.prod(shape))
            names = "abc"[:len(shape)]
            flat = ring[:, slot:slot + 2].rearrange("p s h n -> p (s h n)")[:, 0:n]
            return flat.rearrange(f"p ({' '.join(names)}) -> p {' '.join(names)}",
                                  **{k: v for k, v in zip(names[1:], shape[1:])})

        S0 = L_LOAD + 1
        w_nat = scratch(S0, [P, TAPS])
        w_scaled = scratch(S0 + 2, [TAPS, P])
        w_hi = scratch(S0 + 4, [TAPS, P // 2]).bitcast(F16)
        w_lo = scratch(S0 + 6, [TAPS, P // 2]).bitcast(F16)
        e_nat = scratch(S0 + 8, [BLOCKS, P])
        e_sc = scratch(S0 + 10, [BLOCKS, P])
        diag = scratch(S0 + 12, [BLOCKS, P])
        ones = scratch(S0 + 14, [P])

        ps_conv = [pb(f"ps_conv{h}", [P, CH]) for h in range(2)]
        ps_score = [pb(f"ps_score{k}", [P, CODES]) for k in range(2)]
        ps_idx = pb("ps_idx", [P, CH])
        ps_code = pb("ps_code", [P, CH])
        ps_gn = pb("ps_gn", [P, 512])
        ps_t16 = [ps[:, 0:P // 2].bitcast(F16) for ps in (ps_idx, ps_code)]

        loaded = [sem(f"loaded{h}") for h in range(2)]
        stored = [sem(f"stored{h}") for h in range(2)]
        stat_done = [None, sem("stat1_done"), sem("stat2_done")]
        z32c_done = sem("z32c_done")
        zhc_done = sem("zhc_done")
        zc_done = sem("zc_done")
        hz_done = sem("hz_done")
        hz_used = sem("hz_used")
        conv_done = sem("conv_done")
        x1_done = sem("x1_done")
        z32v_done = sem("z32v_done")
        zhv_done = sem("zhv_done")
        zv_done = sem("zv_done")
        score_done = sem("score_done")
        best_done = sem("best_done")
        place_done = sem("place_done")
        idx_done = sem("idx_done")
        idx_spread = sem("idx_spread")
        row_done = sem("row_done")
        onehot_done = sem("onehot_done")
        code_done = sem("code_done")
        out_done = sem("out_done")
        gn_dve = sem("gn_dve")
        gn_pe = sem("gn_pe")
        gn_act = sem("gn_act")
        gn_ready = [None, sem("gn_ready1"), sem("gn_ready2")]
        in_const, in_w, in_e = sem("in_const"), sem("in_w"), sem("in_e")
        su_dve = sem("su_dve")
        su_pe = sem("su_pe")
        su_pool = sem("su_pool")

        GN_DVE = 11
        xv = x.rearrange("b c (k h r) w -> c b k h (r w)", h=2, r=ROWS)
        ov = out.rearrange("b c (k h r) w -> c b k h (r w)", h=2, r=ROWS)

        def slot(pair, h):
            return ring[:, pair % RING, h, :]

        def gn_turn(k, m):
            if isinstance(m, int) and (k, m) in ((1, 0), (2, IMGS - 1)):
                return 0 if k == 1 else 2 * m + 1
            return 2 * m - 1 if k == 1 else 2 * m + 2

        def hold(eng, s, value):
            if not isinstance(value, int):
                value = eng.to_reg(value)
                eng.wait_ge(su_dve, SU_DONE)
            eng.wait_ge(s, value)

        block = ctx.enter_context(nc.Block())

        @block.sync
        def _(sp):
            sp.dma_start(cst[:, :], const).then_inc(in_const, 16)
            sp.dma_start(w_nat.rearrange("p a b -> p (a b)"),
                         weight.rearrange("o c i j -> o (c i j)")).then_inc(in_w, 16)
            sp.dma_start(e_nat, embedding.rearrange("(b k) c -> k b c", k=P)).then_inc(in_e, 16)

            def load(p, h):
                if not (isinstance(p, int) and p == 0):
                    sp.wait_ge(loaded[h], 16 * p)
                sp.dma_start(slot(p, h), xv[:, p // PPI, p % PPI, h, :]).then_inc(loaded[h], 16)

            def store(p, h):
                sp.wait_ge(out_done, 2 * p + h + 1)
                sp.dma_start(ov[:, p // PPI, p % PPI, h, :], slot(p, h)).then_inc(stored[h], 16)

            for p in range(L_LOAD - L_STAT):
                for h in range(2):
                    load(p, h)

            def pair(t, on, first=False, mid=None):
                for h in range(2):
                    if "stats1" in on and not (isinstance(t, int) and t + L_LOAD >= PAIRS):
                        if "reuse" in on:
                            sp.wait_ge(stored[h], 16 * (t + L_LOAD - RING + 1))
                        load(t + L_LOAD, h)
                    if f"out{h}" in on:
                        store(t - L_VQ if h else t - L_VQ - 1, 1 - h)

            walk_loads(sp, pair, lambda: sp.wait_ge(su_dve, SU_DONE))
            for h in range(2):
                sp.wait_ge(stored[h], 16 * PAIRS)

        @block.scalar
        def _(act):
            def gn(k, m):
                turn = gn_turn(k, m)
                act.wait_ge(gn_dve, GN_DVE * turn + 5)
                nc.scalar.activation(gt[:, 6:7], gt[:, 5:6], ACT.Sqrt).then_inc(gn_act, 1)

            def pair(t, on, first=False, mid=None):
                for h in range(2):
                    if h == 1 and mid is not None:
                        gn(2, mid)
                    n, c = 2 * (t + 1) + h, 2 * (t - L_VQZ) + h
                    w = c - 3
                    if f"out{h}" in on:
                        act.wait_ge(idx_spread, w + 1)
                        if not (isinstance(t, int) and w < 2):
                            act.wait_ge(onehot_done, w - 1)
                        nc.scalar.copy(idx_row[1 - h][:, :], ps_idx[:, :]).then_inc(row_done, 1)
                    if "vqz" in on:
                        act.wait_ge(gn_ready[2], (t - L_VQZ) // PPI + 1)
                        if not (isinstance(t, int) and c < 2):
                            act.wait_ge(zv_done, c - 1)
                        nc.scalar.activation(z32v[h][:, :], slot(t - L_VQZ, h), ACT.Identity,
                                             bias=gn_ab[2][:, 1:2], scale=gn_ab[2][:, 0:1]
                                             ).then_inc(z32v_done, 1)
                        if not (isinstance(t, int) and c < 2):
                            act.wait_ge(score_done, TILES * (c - 1))
                        act.wait_ge(z32v_done, c + 1)
                        nc.scalar.copy(zv[h][:, 0, :], z32v[h][:, :]).then_inc(zhv_done, 1)
                    if "convz" in on and first and h == 0:
                        m = (t + 1) // PPI
                        act.wait_ge(gn_ready[1], m + 1)
                        if not (isinstance(t, int) and t < 0):
                            act.wait_ge(zc_done, 3 * n)
                        tail = slot(t + PPI, 1)[:, (ROWS - HALO) * W:CH]
                        nc.scalar.activation(z32c[0][:, 0:HALO * W], tail, ACT.Identity,
                                             bias=gn_ab[1][:, 1:2], scale=gn_ab[1][:, 0:1]
                                             ).then_inc(hz_done, 1)
                        if not (isinstance(t, int) and t < 0):
                            act.wait_ge(conv_done, n - 1)
                        act.wait_ge(hz_done, 2 * m + 1)
                        nc.scalar.copy(zc[0][:, 0, 0:HALO, HALO:],
                                       z32c[0][:, 0:HALO * W].rearrange("p (r w) -> p r w", w=W)
                                       ).then_inc(hz_done, 1)
                        act.wait_ge(hz_used, m + 1)
                    if "convz" in on:
                        if not (isinstance(t, int) and n < 2) and not (first and h == 0):
                            act.wait_ge(zc_done, 3 * n)
                        nc.scalar.activation(z32c[h][:, :], slot(t + 1, h), ACT.Identity,
                                             bias=gn_ab[1][:, 1:2], scale=gn_ab[1][:, 0:1]
                                             ).then_inc(z32c_done, 1)
                    if "convz" in on:
                        if not (isinstance(t, int) and n < 2):
                            act.wait_ge(conv_done, n - 1)
                        act.wait_ge(z32c_done, n + 1)
                        nc.scalar.copy(zc[h][:, 0, HALO:, HALO:],
                                       z32c[h][:, :].rearrange("p (r w) -> p r w", w=W)
                                       ).then_inc(zhc_done, 1)

            walk(act, pair, gn)

        @block.gpsimd
        def _(pool):
            pool.wait_ge(su_dve, SU_EMAX)
            nc.gpsimd.partition_all_reduce(small[:, 9:10], small[:, 8:9], P,
                                           bass.bass_isa.ReduceOp.max).then_inc(su_pool, 1)

            def pair(t, on, first=False, mid=None):
                for h in range(2):
                    if "vqz" in on:
                        n = 2 * (t - L_VQZ) + h
                        if not (isinstance(t, int) and n < 2):
                            hold(pool, score_done, TILES * (n - 1))
                        hold(pool, zhv_done, n + 1)
                        nc.gpsimd.tensor_tensor(zv[h][:, 1, :], z32v[h][:, :], zv[h][:, 0, :],
                                                ALU.subtract).then_inc(zv_done, 1)
                    if "convz" in on:
                        n = 2 * (t + 1) + h
                        body = z32c[h][:, :].rearrange("p (r w) -> p r w", w=W)
                        if first and h == 0:
                            m = (t + 1) // PPI
                            hold(pool, hz_done, 2 * m + 2)
                            nc.gpsimd.tensor_tensor(
                                zc[0][:, 1, 0:HALO, HALO:],
                                z32c[0][:, 0:HALO * W].rearrange("p (r w) -> p r w", w=W),
                                zc[0][:, 0, 0:HALO, HALO:], ALU.subtract).then_inc(hz_used, 1)
                        elif not (isinstance(t, int) and n < 2):
                            hold(pool, conv_done, n - 1)
                        if not (first and h == 0):
                            hold(pool, zc_done, 3 * n)
                            nc.gpsimd.tensor_copy(zc[h][:, :, 0:HALO, :],
                                                  zc[1 - h][:, :, ROWS:, :]).then_inc(zc_done, 1)
                        hold(pool, zhc_done, n + 1)
                        nc.gpsimd.tensor_tensor(zc[h][:, 1, HALO:, HALO:], body,
                                                zc[h][:, 0, HALO:, HALO:],
                                                ALU.subtract).then_inc(zc_done, 1)
                        if first and h == 0:
                            hold(pool, hz_used, m + 1)
                            hold(pool, zc_done, 3 * n + 1)
                            for rows in (slice(0, HALO), slice(HALO, HALO + ROWS)):
                                nc.gpsimd.tensor_copy(zc[h][:, :, rows, 0:HALO],
                                                      zc[h][:, :, rows, W:]).then_inc(zc_done, 1)
                        else:
                            hold(pool, zc_done, 3 * n + 2)
                            nc.gpsimd.tensor_copy(zc[h][:, :, HALO:, 0:HALO],
                                                  zc[h][:, :, HALO:, W:]).then_inc(zc_done, 1)

            walk(pool, pair, lambda k, m: None)

        @block.tensor
        def _(pe):
            pe.wait_ge(su_dve, SU_SPLIT)
            n = 0
            for tap in range(TAPS):
                for part, src in enumerate((w_hi, w_lo)):
                    if n >= 2:
                        pe.wait_ge(su_dve, SU_SPLIT + n - 1)
                    nc.tensor.transpose(ps_t16[n % 2], src[:, tap, :],
                                        id16[:, :]).then_inc(su_pe, 1)
                    n += 1
            for b in range(BLOCKS):
                for part in range(2):
                    pe.wait_ge(su_dve, SU_SPLIT + n - 1)
                    nc.tensor.transpose(ps_t16[n % 2], eR[:, part, b, :],
                                        id16[:, :]).then_inc(su_pe, 1)
                    n += 1
            for b in range(BLOCKS):
                mm = nc.tensor.matmul(ps_score[0][:, b * P:(b + 1) * P], ones, diag[:, b, :],
                                      start=True, stop=True)
            mm.then_inc(su_pe, 1)
            pe.wait_ge(su_dve, SU_DONE)

            def gn(k, m):
                turn = gn_turn(k, m)
                grp = cst[:, C_GRP:C_GRP + P]
                pe.wait_ge(gn_dve, GN_DVE * turn + 1)
                nc.tensor.matmul(ps_gn[:, 0:2], grp, gt[:, 0:2], start=True, stop=True).then_inc(gn_pe, 1)
                pe.wait_ge(gn_dve, GN_DVE * turn + 4)
                nc.tensor.matmul(ps_gn[:, 2:3], grp, gt[:, 4:5], start=True, stop=True).then_inc(gn_pe, 1)

            products = [(i, j, wp, zp) for i in range(3) for j in range(3)
                        for wp, zp in ((0, 0), (1, 0), (0, 1))]
            cuts = [0, 7, 14, 21, 27]

            def pair(t, on, first=False, mid=None):
                for h in range(2):
                    if h == 1 and mid is not None:
                        gn(2, mid)
                    u, v = 2 * t + h, 2 * (t - L_VQ) + h
                    w = v - 1
                    has_out = f"out{h}" in on
                    for q in range(TILES):
                        if "vq" in on:
                            if q == 0:
                                pe.wait_ge(zv_done, v + 1)
                            if not (isinstance(t, int) and TILES * v + q < 2):
                                pe.wait_ge(best_done, TILES * v + q - 1)
                            tile = slice(q * P, (q + 1) * P)
                            ps = ps_score[q % 2][:, :]
                            nc.tensor.matmul(ps, zv[h][:, 0, tile], eT[:, 0, :], start=True, stop=False)
                            nc.tensor.matmul(ps, zv[h][:, 0, tile], eT[:, 1, :], start=False, stop=False)
                            nc.tensor.matmul(ps, zv[h][:, 1, tile], eT[:, 0, :],
                                             start=False, stop=True).then_inc(score_done, 1)
                        if "conv" in on:
                            if q == 0:
                                pe.wait_ge(zc_done, 3 * (u + 1))
                                if not (isinstance(t, int) and u < 2):
                                    pe.wait_ge(x1_done, u - 1)
                            for n in range(cuts[q], cuts[q + 1]):
                                i, j, wp, zp = products[n]
                                mm = nc.tensor.matmul(
                                    ps_conv[h][:, :].rearrange("p (r w) -> p r w", w=W),
                                    wT[:, wp, 3 * i + j, :],
                                    zc[h][:, zp, HALO - i:HALO - i + ROWS, HALO - j:HALO - j + W],
                                    start=(n == 0), stop=(n == len(products) - 1))
                            if q == TILES - 1:
                                mm.then_inc(conv_done, 1)
                        if has_out and q == 0:
                            pe.wait_ge(idx_done, w + 1)
                            if not (isinstance(t, int) and w < 1):
                                pe.wait_ge(row_done, w)
                            for r in range(TILES):
                                mm = nc.tensor.matmul(ps_idx[:, r * P:(r + 1) * P],
                                                      idx16[1 - h][:, r:r + 1].to_broadcast([P, P]),
                                                      id16[:, :], start=True, stop=True)
                            mm.then_inc(idx_spread, 1)
                        if has_out and q == 2:
                            pe.wait_ge(onehot_done, w + 1)
                            if not (isinstance(t, int) and w < 1):
                                pe.wait_ge(out_done, w)
                            for b in range(BLOCKS):
                                for part in range(2):
                                    mm = nc.tensor.matmul(
                                        ps_code[:, :], eR[:, part, b, :], onehot[1 - h][:, b, :],
                                        start=(b == 0 and part == 0),
                                        stop=(b == BLOCKS - 1 and part == 1))
                            mm.then_inc(code_done, 1)

            walk(pe, pair, gn)

        @block.vector
        def _(dve):
            v = nc.vector
            steps = [0]

            def link(ins):
                steps[0] += 1
                ins.then_inc(su_dve, 1)
                dve.wait_ge(su_dve, steps[0])

            dve.wait_ge(in_w, 16)
            link(v.tensor_reduce(small[:, 4:5], w_nat.rearrange("p a b -> p (a b)"), AX.X, ALU.max,
                                 apply_absolute_value=True))
            dve.wait_ge(in_e, 16)
            link(v.tensor_reduce(small[:, 5:6], e_nat.rearrange("p a b -> p (a b)"), AX.X, ALU.max,
                                 apply_absolute_value=True))
            link(v.tensor_copy(small[:, 8:9], small[:, 5:6]))
            assert steps[0] == SU_EMAX
            dve.wait_ge(su_pool, 1)
            link(v.tensor_copy(small[:, 5:6], small[:, 9:10]))
            link(v.tensor_scalar(small[:, 4:6], small[:, 4:6], 2.0 ** -100, 2.0 ** 100, ALU.max, ALU.min))
            link(v.tensor_scalar(small[:, 10:12].bitcast(I32), small[:, 4:6].bitcast(I32), 0x7F800000,
                                 None, ALU.bitwise_and))
            link(v.reciprocal(small[:, 6:8], small[:, 10:12]))
            link(v.tensor_scalar(small[:, 6:8], small[:, 6:8], WS, None, ALU.mult))
            link(v.tensor_scalar(conv_scale, small[:, 10:11], 1.0 / (WS * ZS), None, ALU.mult))
            link(v.tensor_scalar(code_scale, small[:, 11:12], 1.0 / WS, None, ALU.mult))
            link(v.tensor_scalar(small[:, 2:3], small[:, 11:12], -0.5 * ZS / WS, None, ALU.mult))
            link(v.tensor_scalar(w_scaled, w_nat.rearrange("p c t -> p t c"), small[:, 6:7], None, ALU.mult))
            link(v.tensor_copy(w_hi, w_scaled))
            link(v.tensor_tensor(w_lo, w_scaled, w_hi, ALU.subtract))
            link(v.tensor_scalar(e_sc, e_nat, small[:, 7:8], None, ALU.mult))
            link(v.tensor_copy(eR[:, 0], e_sc))
            link(v.tensor_tensor(eR[:, 1], e_sc, eR[:, 0], ALU.subtract))
            link(v.tensor_tensor(e_nat, e_sc, e_sc, ALU.mult))
            link(v.tensor_reduce(small[:, 12:16], e_nat, AX.X, ALU.add))
            dve.wait_ge(in_const, 16)
            for b in range(BLOCKS):
                link(v.tensor_scalar(diag[:, b, :], cst[:, C_ID:C_ID + P], small[:, 12 + b:13 + b],
                                     None, ALU.mult))
            link(v.memset(ones, 1.0))
            link(v.memset(best[0][:, :], 3.0e38))
            link(v.memset(best[1][:, :], 3.0e38))
            link(v.tensor_copy(id16[:, :], cst[:, C_ID:C_ID + P]))
            assert steps[0] == SU_SPLIT
            n = 0
            for tap in range(TAPS):
                for part in range(2):
                    dve.wait_ge(su_pe, n + 1)
                    v.tensor_copy(wT[:, part, tap, :], ps_t16[n % 2]
                                  ).then_inc(su_dve, 1)
                    n += 1
            for b in range(BLOCKS):
                for part in range(2):
                    dve.wait_ge(su_pe, n + 1)
                    v.tensor_copy(eT[:, part, b * P:(b + 1) * P], ps_t16[n % 2]
                                  ).then_inc(su_dve, 1)
                    n += 1
            dve.wait_ge(su_pe, n + 1)
            v.tensor_scalar(code_bias[:, :], ps_score[0][:, :], small[:, 2:3], None,
                            ALU.mult).then_inc(su_dve, 1)
            dve.wait_ge(su_dve, SU_DONE)

            def gn(k, m):
                turn = gn_turn(k, m)
                at = [0]

                def link(ins):
                    at[0] += 1
                    ins.then_inc(gn_dve, 1)
                    hold(dve, gn_dve, GN_DVE * turn + at[0])

                hold(dve, stat_done[k], CPI * (m + 1))
                link(v.bn_aggr(gt[:, 0:2], stat[k][:, :, :].rearrange("p c s -> p (c s)")))
                hold(dve, gn_pe, 2 * turn + 1)
                link(v.tensor_copy(gt[:, 8:10], ps_gn[:, 0:2]))
                link(v.scalar_tensor_tensor(gt[:, 3:4], gt[:, 8:9], -1.0, gt[:, 0:1],
                                            ALU.mult, ALU.add))
                link(v.tensor_tensor(gt[:, 4:5], gt[:, 3:4], gt[:, 3:4], ALU.mult))
                hold(dve, gn_pe, 2 * turn + 2)
                link(v.scalar_tensor_tensor(gt[:, 5:6], ps_gn[:, 2:3], EPS, gt[:, 9:10],
                                            ALU.add, ALU.add))
                hold(dve, gn_act, turn + 1)
                link(v.reciprocal(gt[:, 7:8], gt[:, 6:7]))
                link(v.tensor_tensor(gt[:, 10:11], gt[:, 7:8], gt[:, 7:8], ALU.mult))
                link(v.tensor_tensor(gt[:, 11:12], gt[:, 10:11], gt[:, 5:6], ALU.mult))
                link(v.tensor_scalar(gt[:, 12:13], gt[:, 11:12], -0.5, 1.5, ALU.mult, ALU.add))
                link(v.tensor_tensor(gt[:, 13:14], gt[:, 12:13], gt[:, 7:8], ALU.mult))
                if not (isinstance(m, int) and m == 0):
                    hold(dve, z32c_done if k == 1 else z32v_done, CPI * m)
                link(v.tensor_scalar(gn_ab[k][:, 0:1], gt[:, 13:14], ZS, None, ALU.mult))
                assert at[0] == GN_DVE
                v.scalar_tensor_tensor(gn_ab[k][:, 1:2], gt[:, 8:9], -1.0, gn_ab[k][:, 0:1],
                                       ALU.mult, ALU.mult).then_inc(gn_ready[k], 1)

            def pair(t, on, first=False, mid=None):
                for h in range(2):
                    if h == 1 and mid is not None:
                        gn(2, mid)
                    u, c = 2 * t + h, 2 * (t - L_VQ) + h
                    w = c - 1
                    has_out = f"out{h}" in on

                    def top(q):
                        if "vq" not in on:
                            return
                        hold(dve, score_done, TILES * c + q + 1)
                        if not (isinstance(t, int) and TILES * c + q < 2):
                            hold(dve, place_done, TILES * c + q - 1)
                        v.tensor_tensor_reduce(scores[q % 2][:, :], ps_score[q % 2][:, :],
                                               code_bias[:, :], 1.0, -3.0e38, ALU.add, ALU.max,
                                               best[q % 2][:, 0:1]).then_inc(best_done, 1)

                    def find(q):
                        if "vq" not in on:
                            return
                        hold(dve, best_done, TILES * c + q + 1)
                        v.max_index(place[h][:, q, :], best[q % 2][:, :],
                                    scores[q % 2][:, :]).then_inc(place_done, 1)

                    top(0)
                    if f"evac{h}" in on:
                        e = u - 1
                        x1 = slot(t if h else t - 1, 1 - h)
                        hold(dve, conv_done, e + 1)
                        v.scalar_tensor_tensor(x1, ps_conv[1 - h][:, :], conv_scale, x1,
                                               ALU.mult, ALU.add).then_inc(x1_done, 1)
                    top(1)
                    find(0)
                    if f"evac{h}" in on:
                        hold(dve, x1_done, e + 1)
                        v.bn_stats(stat[2][:, e % CPI, :], x1).then_inc(stat_done[2], 1)
                    if has_out:
                        hold(dve, row_done, w + 1)
                        if not (isinstance(t, int) and w < 2):
                            hold(dve, code_done, w - 1)
                        for b in range(BLOCKS):
                            last = v.tensor_scalar(onehot[1 - h][:, b, :], idx_row[1 - h][:, :],
                                                   cst[:, C_CODE + b:C_CODE + b + 1], None,
                                                   ALU.is_equal)
                        last.then_inc(onehot_done, 1)
                    top(2)
                    find(1)
                    if "stats1" in on:
                        p = t + L_STAT
                        hold(dve, loaded[h], 16 * (p + 1))
                        v.bn_stats(stat[1][:, (2 * p + h) % CPI, :], slot(p, h)
                                   ).then_inc(stat_done[1], 1)
                    top(3)
                    find(2)
                    if has_out:
                        hold(dve, code_done, w + 1)
                        y = slot(t - L_VQ if h else t - L_VQ - 1, 1 - h)
                        v.scalar_tensor_tensor(y, ps_code[:, :], code_scale, y,
                                               ALU.mult, ALU.add).then_inc(out_done, 1)
                    find(3)
                    if "vq" in on:
                        hold(dve, place_done, TILES * (c + 1))
                        if not (isinstance(t, int) and c < 2):
                            hold(dve, idx_spread, c - 1)
                        v.tensor_copy(idx16[h][:, :], place[h][:, :, 0]).then_inc(idx_done, 1)

            walk(dve, pair, gn)


SU_EMAX = 3
SU_SPLIT = 27
SU_DONE = SU_SPLIT + 2 * (TAPS + BLOCKS) + 1


def walk_loads(sp, pair, setup_over):
    with sp.Fori(0, L_STAT) as i:
        pair(i - L_STAT, {"stats1"})
    setup_over()
    with sp.Fori(0, 18) as t:
        pair(t, {"stats1"})
    pair(18, {"stats1", "out1"})
    for t in range(19, 21):
        pair(t, {"stats1", "out0", "out1"})
    with sp.Fori(21, PAIRS - L_LOAD) as t:
        pair(t, {"stats1", "out0", "out1", "reuse"})
    with sp.Fori(PAIRS - L_LOAD, PAIRS + L_VQ) as t:
        pair(t, {"out0", "out1"})
    pair(PAIRS + L_VQ, {"out0"})


def kernel(x, L0_conv_weight, L1_conv_embedding):
    import concourse.bacc as bacc
    from concourse.bass_utils import run_bass_kernel_spmd

    nc = bacc.Bacc("TRN2", target_bir_lowering=False, num_devices=1)
    arrays, args = {}, []
    for name, a in (("x", x), ("weight", L0_conv_weight), ("embedding", L1_conv_embedding),
                    ("const", constants())):
        a = np.ascontiguousarray(a)
        arrays[f"in_{name}"] = a
        args.append(nc.dram_tensor(f"in_{name}", a.shape, mybir.dt.from_np(a.dtype),
                                   kind="ExternalInput").ap())
    args.append(nc.dram_tensor("out_0", x.shape, F32, kind="ExternalOutput").ap())
    program(nc, *args)
    r = run_bass_kernel_spmd(nc, [arrays], core_ids=[0])
    return r.results[0]["out_0"]
```

```python
from contextlib import ExitStack

import numpy as np

import concourse.bass as bass
from concourse import mybir

F32 = mybir.dt.float32
F16 = mybir.dt.float16
I32 = mybir.dt.int32
U32 = mybir.dt.uint32
ALU = mybir.AluOpType
ACT = mybir.ActivationFunctionType
AX = mybir.AxisListType

P = 128
IMGS, H, W = 16, 128, 128
CODES = 512
BLOCKS = CODES // P
TAPS = 9
SEGS = 4
KW = 3
PROW = 2
COUPLES = 2 * PROW
ROWS = 4
CH = ROWS * W
TILES = CH // P
CPI = H // ROWS
PPI = CPI // 2
PAIRS = IMGS * PPI
HALO = 2
GROUP = 4
EPS = 1e-5

L_STAT = PPI + 1
L_LOAD = L_STAT + 1
L_VQZ = PPI + 1
L_VQ = L_VQZ + 1
L_OUT = L_VQ + 1
RING = L_LOAD + L_VQ + 2

ZS = 64.0
WS = 256.0

C_ID, C_GRP, C_CODE = 0, P, 2 * P
C_ALL = 2 * P + BLOCKS


def constants():
    c = np.zeros((P, C_ALL), np.float32)
    c[:, C_ID:C_ID + P] = np.eye(P)
    c[:, C_GRP:C_GRP + P] = np.kron(np.eye(P // GROUP), np.full((GROUP, GROUP), 1.0 / GROUP))
    c[:, C_CODE:C_CODE + BLOCKS] = np.arange(P)[:, None] + P * np.arange(BLOCKS)[None, :]
    return c


def walk(eng, pair, gn):
    def span(lo, hi, on):
        with eng.Fori(lo, hi) as t:
            pair(t, on)

    front = {"stats1"}
    conv = {"stats1", "convz", "conv", "end"}
    full = conv | {"vqz", "vq", "idx0", "idx1", "out0", "out1"}
    pair(-L_STAT, front)
    with eng.Fori(1, L_STAT - 1) as i:
        pair(i - L_STAT, front)
    gn(1, 0, -1)
    pair(-1, {"stats1", "convz"}, first=True)
    pair(0, conv - {"end"})
    pair(1, conv)
    span(2, 15, conv)
    gn(1, 1, 15)
    pair(15, conv, first=True)
    pair(16, conv)
    gn(2, 0, 17)
    pair(17, conv | {"vqz"})
    pair(18, conv | {"vqz", "vq", "idx1"})
    pair(19, full)
    span(20, 31, full)
    with eng.Fori(1, IMGS - 2) as j:
        gn(1, j + 1, PPI * j + 15)
        pair(PPI * j + 15, full, first=True)
        pair(PPI * j + 16, full)
        gn(2, j, PPI * j + 17)
        with eng.Fori(PPI * j + 17, PPI * j + 31) as t:
            pair(t, full)
    late = full - {"stats1"}
    j = IMGS - 2
    gn(1, j + 1, PPI * j + 15)
    pair(PPI * j + 15, late, first=True)
    pair(PPI * j + 16, late)
    gn(2, j, PPI * j + 17)
    span(PPI * j + 17, PPI * j + 31, late)
    pair(PAIRS - 1, late - {"convz"})
    tail = {"vqz", "vq", "idx0", "idx1", "out0", "out1"}
    pair(PAIRS, tail | {"end"})
    gn(2, IMGS - 1, PAIRS + 1)
    span(PAIRS + 1, PAIRS + L_VQZ, tail)
    pair(PAIRS + L_VQZ, tail - {"vqz"})
    pair(PAIRS + L_VQ, {"idx0", "out0", "out1"})


def program(nc, x, weight, embedding, const, out):
    ctx = ExitStack()
    with ctx:
        def sb(name, shape, dt=F32):
            return ctx.enter_context(nc.sbuf_tensor(name, shape, dt))

        def pb(name, shape, dt=F32):
            return ctx.enter_context(nc.psum_tensor(name, shape, dt))

        def sem(name):
            return ctx.enter_context(nc.semaphore(name))

        ring = sb("ring", [P, RING, COUPLES, 2, W])
        cst = sb("cst", [P, C_ALL])
        id16 = sb("id16", [P, P], F16)
        wT = sb("wT", [P, 2, SEGS * KW, P], F16)
        eT = sb("eT", [P, 2, CODES], F16)
        eR = sb("eR", [P, 2, BLOCKS, P], F16)
        code_bias = sb("code_bias", [P, CODES])
        zb = sb("zb", [P, 2 * COUPLES + HALO, W + HALO])
        t32 = [sb(f"t32{k}", [P, COUPLES, W + HALO]) for k in range(2)]
        th = sb("th", [P, 2, SEGS, COUPLES, W + HALO], F16)
        m1 = sb("m1", [P, COUPLES, W])
        junk = [sb(f"junk{n}", [P, 2 * CH], mybir.dt.bfloat16) for n in range(2)]
        z32v = [sb(f"z32v{h}", [P, CH]) for h in range(2)]
        zv = [sb(f"zv{h}", [P, 2, CH], F16) for h in range(2)]
        scores = [sb(f"scores{k}", [P, CODES]) for k in range(2)]
        best = [sb(f"best{k}", [P, 8]) for k in range(2)]
        place = [sb(f"place{h}", [P, TILES, 8], U32) for h in range(2)]
        idx16 = [sb(f"idx16{h}", [P, TILES], F16) for h in range(2)]
        idx_row = [sb(f"idx_row{h}", [P, CH], F16) for h in range(2)]
        onehot = sb("onehot", [P, BLOCKS, CH], F16)
        stat = [None, sb("stat1", [P, 2, PPI, 1]), sb("stat2", [P, 2, PPI, 1])]
        neg_shift = [None, sb("neg_shift1", [P, 1]), sb("neg_shift2", [P, 1])]
        next_shift = sb("next_shift", [P, 1])
        gn_ab = [None, sb("gn_ab1", [P, 2]), sb("gn_ab2", [P, 2])]
        gt = sb("gt", [P, 16])
        small = sb("small", [P, 16])
        conv_scale = small[:, 0:1]
        code_scale = small[:, 1:2]
        neg_conv_scale = small[:, 3:4]

        def scratch(slot, shape):
            n = int(np.prod(shape))
            names = "abc"[:len(shape)]
            flat = ring[:, slot:slot + 2].rearrange("p s c e w -> p (s c e w)")[:, 0:n]
            return flat.rearrange(f"p ({' '.join(names)}) -> p {' '.join(names)}",
                                  **{k: v for k, v in zip(names[1:], shape[1:])})

        S0 = L_LOAD + 1
        w_nat = scratch(S0, [P, TAPS])
        w_scaled = scratch(S0 + 2, [TAPS, P])
        w_hi = scratch(S0 + 4, [SEGS * KW, P // 2]).bitcast(F16)
        w_lo = scratch(S0 + 6, [SEGS * KW, P // 2]).bitcast(F16)
        w_seg = scratch(S0 + 16, [SEGS * KW, P])
        e_nat = scratch(S0 + 8, [BLOCKS, P])
        e_sc = scratch(S0 + 10, [BLOCKS, P])
        diag = scratch(S0 + 12, [BLOCKS, P])
        ones = scratch(S0 + 14, [P])

        ps_m = [pb(f"ps_m{s}", [P, CH]) for s in range(SEGS)]
        ps_score = [pb(f"ps_score{k}", [P, CODES]) for k in range(2)]
        ps_idx = pb("ps_idx", [P, CH])
        ps_code = pb("ps_code", [P, CH])
        ps_gn = ps_idx
        ps_t16 = [ps[:, 0:P // 2].bitcast(F16) for ps in (ps_idx, ps_code)]

        loaded = [sem(f"loaded{h}") for h in range(2)]
        stored = [sem(f"stored{h}") for h in range(2)]
        stat_done = [None, sem("stat1_done"), sem("stat2_done")]
        zb_done = sem("zb_done")
        t32_done = sem("t32_done")
        thi_done = sem("thi_done")
        th_done = sem("th_done")
        seg_done = sem("seg_done")
        m1_done = sem("m1_done")
        xm_done = sem("xm_done")
        x1_done = sem("x1_done")
        shift_done = sem("shift_done")
        z32v_done = sem("z32v_done")
        zhv_done = sem("zhv_done")
        zv_done = sem("zv_done")
        score_done = sem("score_done")
        best_done = sem("best_done")
        place_done = sem("place_done")
        idx_done = sem("idx_done")
        idx_spread = sem("idx_spread")
        row_done = sem("row_done")
        onehot_done = sem("onehot_done")
        code_done = sem("code_done")
        out_done = sem("out_done")
        gn_dve = sem("gn_dve")
        gn_pe = sem("gn_pe")
        gn_act = sem("gn_act")
        gn_ready = [None, sem("gn_ready1"), sem("gn_ready2")]
        in_const, in_w, in_e = sem("in_const"), sem("in_w"), sem("in_e")
        su_dve = sem("su_dve")
        su_pe = sem("su_pe")
        su_pool = sem("su_pool")

        GN_DVE = 16
        GN_MEANS, GN_DIST, GN_VAR = 5, 8, 9
        xv = x.rearrange("b c (k h r) w -> c b k h (r w)", h=2, r=ROWS)
        ov = out.rearrange("b c (k h r) w -> c b k h (r w)", h=2, r=ROWS)

        def pixels(pair):
            return ring[:, pair % RING, :, :, :].rearrange("p c e w -> p (c e w)")

        def slot(pair, h):
            return pixels(pair)[:, h * CH:(h + 1) * CH]

        def rows(pair, e):
            return ring[:, pair % RING, :, e, :]

        d = [zb[:, 2 * (i // 2):2 * (i // 2) + 2 * COUPLES, :].rearrange(
            "p (k e) w -> p k e w", e=2)[:, :, i % 2, :] for i in range(4)]
        seg_input = [(d[1], d[2], ALU.add), (d[2], d[1], ALU.subtract),
                     (d[0], d[2], ALU.subtract), (d[1], d[3], ALU.subtract)]

        def couples(ps):
            return ps[:, :].rearrange("p (k w) -> p k w", w=W)

        def gn_turn(k, m):
            if isinstance(m, int) and (k, m) in ((1, 0), (2, IMGS - 1)):
                return 0 if k == 1 else 2 * m + 1
            return 2 * m - 1 if k == 1 else 2 * m + 2

        def hold(eng, s, value):
            if not isinstance(value, int):
                value = eng.to_reg(value)
                eng.wait_ge(in_const, 16)
            eng.wait_ge(s, value)

        block = ctx.enter_context(nc.Block())

        @block.sync
        def _(sp):
            sp.dma_start(cst[:, :], const).then_inc(in_const, 16)
            sp.dma_start(w_nat.rearrange("p a b -> p (a b)"),
                         weight.rearrange("o c i j -> o (c i j)")).then_inc(in_w, 16)
            sp.dma_start(e_nat, embedding.rearrange("(b k) c -> k b c", k=P)).then_inc(in_e, 16)

            def load(p, h):
                if not (isinstance(p, int) and p == 0):
                    sp.wait_ge(loaded[h], 16 * p)
                sp.dma_start(slot(p, h), xv[:, p // PPI, p % PPI, h, :]).then_inc(loaded[h], 16)

            def store(p, h):
                values = 2 * p + h + 1, 16 * p
                if not isinstance(p, int):
                    values = [sp.to_reg(n) for n in values]
                sp.wait_ge(out_done, values[0])
                if not (isinstance(p, int) and p == 0):
                    sp.wait_ge(stored[h], values[1])
                sp.dma_start(ov[:, p // PPI, p % PPI, h, :], slot(p, h)).then_inc(stored[h], 16)

            for p in range(L_LOAD - L_STAT):
                for h in range(2):
                    load(p, h)

            def pair(t, on, first=False):
                for h in range(2):
                    if "stats1" in on and not (isinstance(t, int) and t + L_LOAD >= PAIRS):
                        if "reuse" in on:
                            sp.wait_ge(stored[h], 16 * (t + L_LOAD - RING + 1))
                        load(t + L_LOAD, h)
                    if f"out{h}" in on:
                        store(t - L_OUT, h)

            walk_loads(sp, pair, lambda: sp.wait_ge(su_dve, SU_DONE))
            for h in range(2):
                sp.wait_ge(stored[h], 16 * PAIRS)

        @block.scalar
        def _(act):
            def gn(k, m, t):
                turn = gn_turn(k, m)
                hold(act, gn_dve, GN_DVE * turn + GN_VAR)
                nc.scalar.activation(gt[:, 6:7], gt[:, 5:6], ACT.Sqrt).then_inc(gn_act, 1)

            def shift1(p):
                hold(act, loaded[0], 16 * (p + 1))
                nc.scalar.mul(neg_shift[1][:, :], pixels(p)[:, 0:1], -1.0).then_inc(shift_done, 1)
                hold(act, shift_done, p // PPI + 1)

            def stats(k, p, last):
                for k0, p0 in last:
                    hold(act, stat_done[k0], 2 * (p0 + 1))
                for n, func in enumerate((ACT.Identity, ACT.Square)):
                    nc.scalar.activation(junk[n][:, :], pixels(p), func, bias=neg_shift[k][:, :],
                                         accum_out=stat[k][:, n, p % PPI, :]
                                         ).then_inc(stat_done[k], 1)

            def row(t, h):
                if f"idx{h}" in row.on:
                    w = 2 * (t - L_VQ) + h - 1
                    hold(act, idx_spread, w + 1)
                    if not (isinstance(t, int) and w < 2):
                        hold(act, onehot_done, w - 1)
                    nc.scalar.copy(idx_row[1 - h][:, :], ps_idx[:, :]).then_inc(row_done, 1)

            scalars = dict(bias=gn_ab[1][:, 1:2], scale=gn_ab[1][:, 0:1])

            def z_halo(t, first):
                p = t + 1
                if first:
                    hold(act, gn_ready[1], p // PPI + 1)
                if not (isinstance(t, int) and p == 0):
                    hold(act, t32_done, SEGS * p)
                    hold(act, zb_done, 3 * p)
                if first:
                    last = ring[:, (p + PPI - 1) % RING, COUPLES - 1, :, :]
                    nc.scalar.activation(zb[:, 0:HALO, HALO:], last, ACT.Identity,
                                         **scalars).then_inc(zb_done, 1)
                else:
                    nc.scalar.copy(zb[:, 0:HALO, :], zb[:, 2 * COUPLES:, :]).then_inc(zb_done, 1)

            def z_rows(t, first):
                p = t + 1
                hold(act, zb_done, 3 * p + 1)
                nc.scalar.activation(zb[:, HALO:, HALO:],
                                     pixels(p).rearrange("p (r w) -> p r w", w=W), ACT.Identity,
                                     **scalars).then_inc(zb_done, 1)
                hold(act, zb_done, 3 * p + 2)
                r0 = 0 if first else HALO
                nc.scalar.copy(zb[:, r0:, 0:HALO], zb[:, r0:, W:]).then_inc(zb_done, 1)

            def hi(t, s):
                n = SEGS * (t + 1) + s
                hold(act, t32_done, n + 1)
                if not (isinstance(t, int) and t < 0):
                    hold(act, seg_done, n - SEGS + 1)
                nc.scalar.copy(th[:, 0, s, :, :], t32[s % 2][:, :, :]).then_inc(thi_done, 1)

            def z_vq(t, h):
                c = 2 * (t - L_VQZ) + h
                hold(act, gn_ready[2], (t - L_VQZ) // PPI + 1)
                if not (isinstance(t, int) and c < 2):
                    hold(act, zv_done, c - 1)
                nc.scalar.activation(z32v[h][:, :], slot(t - L_VQZ, h), ACT.Identity,
                                     bias=gn_ab[2][:, 1:2], scale=gn_ab[2][:, 0:1]
                                     ).then_inc(z32v_done, 1)

            def hi_vq(t, h):
                c = 2 * (t - L_VQZ) + h
                if not (isinstance(t, int) and c < 2):
                    hold(act, score_done, TILES * (c - 1))
                hold(act, z32v_done, c + 1)
                nc.scalar.copy(zv[h][:, 0, :], z32v[h][:, :]).then_inc(zhv_done, 1)

            def pair(t, on, first=False):
                row.on = on
                if "convz" in on:
                    z_halo(t, first)
                if "convz" in on:
                    z_rows(t, first)
                row(t, 0)
                if "conv" in on:
                    hold(act, seg_done, SEGS * t + 1)
                    if not (isinstance(t, int) and t < 1):
                        hold(act, xm_done, 2 * t)
                    nc.scalar.mul(m1[:, :, :], couples(ps_m[0]), conv_scale).then_inc(m1_done, 1)
                if "convz" in on:
                    hi(t, 0)
                if "end" in on:
                    hold(act, x1_done, 4 * t)
                    if "vqz" in on:
                        hold(act, gn_ready[2], (t - 1) // PPI)
                    stats(2, t - 1, [(1, t - 1 + L_STAT)] if "stats1" in on
                          else [(1, PAIRS - 1), (2, t - 2)])
                if "vqz" in on:
                    z_vq(t, 0)
                if "convz" in on:
                    hi(t, 1)
                if "vqz" in on:
                    hi_vq(t, 0)
                row(t, 1)
                if "convz" in on:
                    hi(t, 2)
                if "stats1" in on:
                    p = t + L_STAT
                    if first:
                        shift1(p)
                    for h in range(2):
                        hold(act, loaded[h], 16 * (p + 1))
                    stats(1, p, [(2, t - 1)] if "end" in on else
                          [] if isinstance(p, int) and p == 0 else [(1, p - 1)])
                if "vqz" in on:
                    z_vq(t, 1)
                    hi_vq(t, 1)
                if "convz" in on:
                    hi(t, 3)

            shift1(0)
            walk(act, pair, gn)

        @block.gpsimd
        def _(pool):
            pool.wait_ge(su_dve, SU_EMAX)
            nc.gpsimd.partition_all_reduce(small[:, 9:10], small[:, 8:9], P,
                                           bass.bass_isa.ReduceOp.max).then_inc(su_pool, 1)

            def transform(t, s):
                p = t + 1
                if s == 0:
                    hold(pool, zb_done, 3 * (p + 1))
                n = SEGS * p + s
                if not (isinstance(n, int) and n < 2):
                    hold(pool, th_done, n - 1)
                a, b, op = seg_input[s]
                nc.gpsimd.tensor_tensor(t32[s % 2][:, :, :], a, b, op).then_inc(t32_done, 1)

            def lo(t, s):
                hold(pool, thi_done, SEGS * (t + 1) + s + 1)
                nc.gpsimd.tensor_tensor(th[:, 1, s, :, :], t32[s % 2][:, :, :], th[:, 0, s, :, :],
                                        ALU.subtract).then_inc(th_done, 1)

            def lo_vq(t, h):
                hold(pool, zhv_done, 2 * (t - L_VQZ) + h + 1)
                nc.gpsimd.tensor_tensor(zv[h][:, 1, :], z32v[h][:, :], zv[h][:, 0, :],
                                        ALU.subtract).then_inc(zv_done, 1)

            def pair(t, on, first=False):
                if "convz" in on:
                    transform(t, 0)
                    transform(t, 1)
                    lo(t, 0)
                if "conv" in on:
                    hold(pool, m1_done, t + 1)
                    for e in range(2):
                        nc.gpsimd.tensor_tensor(rows(t, e), rows(t, e), m1[:, :, :],
                                                ALU.add).then_inc(xm_done, 1)
                if "convz" in on:
                    transform(t, 2)
                    lo(t, 1)
                if "vqz" in on:
                    lo_vq(t, 0)
                if "convz" in on:
                    transform(t, 3)
                    lo(t, 2)
                if "vqz" in on:
                    lo_vq(t, 1)
                if "convz" in on:
                    lo(t, 3)

            walk(pool, pair, lambda k, m, t: None)

        @block.tensor
        def _(pe):
            pe.wait_ge(su_dve, SU_SPLIT)
            n = 0
            for tap in range(SEGS * KW):
                for part, src in enumerate((w_hi, w_lo)):
                    if n >= 2:
                        pe.wait_ge(su_dve, SU_SPLIT + n - 1)
                    nc.tensor.transpose(ps_t16[n % 2], src[:, tap, :],
                                        id16[:, :]).then_inc(su_pe, 1)
                    n += 1
            for b in range(BLOCKS):
                for part in range(2):
                    pe.wait_ge(su_dve, SU_SPLIT + n - 1)
                    nc.tensor.transpose(ps_t16[n % 2], eR[:, part, b, :],
                                        id16[:, :]).then_inc(su_pe, 1)
                    n += 1
            for b in range(BLOCKS):
                mm = nc.tensor.matmul(ps_score[0][:, b * P:(b + 1) * P], ones, diag[:, b, :],
                                      start=True, stop=True)
            mm.then_inc(su_pe, 1)
            pe.wait_ge(su_dve, SU_DONE)

            gn_read = []

            def gn(k, m, t):
                turn = gn_turn(k, m)
                grp = cst[:, C_GRP:C_GRP + P]
                pe.wait_ge(gn_dve, GN_DVE * turn + GN_MEANS)
                if not (isinstance(t, int) and t <= L_VQ):
                    pe.wait_ge(row_done, 2 * (t - L_VQ) - 1)
                nc.tensor.matmul(ps_gn[:, 0:2], grp, gt[:, 0:2], start=True, stop=True).then_inc(gn_pe, 1)
                pe.wait_ge(gn_dve, GN_DVE * turn + GN_DIST)
                nc.tensor.matmul(ps_gn[:, 2:3], grp, gt[:, 4:5], start=True, stop=True).then_inc(gn_pe, 1)
                gn_read[:] = [GN_DVE * turn + GN_VAR]

            products = [(j, wp, zp) for j in range(KW) for wp, zp in ((0, 0), (1, 0), (0, 1))]

            def segment(t, s, part):
                if part == 0:
                    pe.wait_ge(th_done, SEGS * t + s + 1)
                    if not (isinstance(t, int) and t < 1):
                        if s == 0:
                            pe.wait_ge(m1_done, t)
                        else:
                            pe.wait_ge(x1_done, 4 * (t - 1) + s + 1)
                for n in (range(5), range(5, len(products)))[part]:
                    j, wp, zp = products[n]
                    mm = nc.tensor.matmul(couples(ps_m[s]), wT[:, wp, KW * s + j, :],
                                          th[:, zp, s, :, HALO - j:HALO - j + W],
                                          start=(n == 0), stop=(n == len(products) - 1))
                if part:
                    mm.then_inc(seg_done, 1)

            def pair(t, on, first=False):
                for h in range(2):
                    v = 2 * (t - L_VQ) + h
                    w = v - 1
                    for q in range(TILES):
                        if "vq" in on:
                            if q == 0:
                                pe.wait_ge(zv_done, v + 1)
                            if not (isinstance(t, int) and TILES * v + q < 2):
                                pe.wait_ge(best_done, TILES * v + q - 1)
                            tile = slice(q * P, (q + 1) * P)
                            ps = ps_score[q % 2][:, :]
                            nc.tensor.matmul(ps, zv[h][:, 0, tile], eT[:, 0, :], start=True, stop=False)
                            nc.tensor.matmul(ps, zv[h][:, 0, tile], eT[:, 1, :], start=False, stop=False)
                            nc.tensor.matmul(ps, zv[h][:, 1, tile], eT[:, 0, :],
                                             start=False, stop=True).then_inc(score_done, 1)
                        if "conv" in on:
                            segment(t, 2 * h + q // 2, q % 2)
                        if f"out{h}" in on and q == 0:
                            y = w - 1
                            pe.wait_ge(onehot_done, y + 1)
                            if not (isinstance(t, int) and y < 1):
                                pe.wait_ge(out_done, y)
                            for b in range(BLOCKS):
                                for part in range(2):
                                    mm = nc.tensor.matmul(
                                        ps_code[:, :], eR[:, part, b, :], onehot[:, b, :],
                                        start=(b == 0 and part == 0),
                                        stop=(b == BLOCKS - 1 and part == 1))
                            mm.then_inc(code_done, 1)
                        if f"idx{h}" in on and q == 1:
                            pe.wait_ge(idx_done, w + 1)
                            if gn_read:
                                pe.wait_ge(gn_dve, gn_read.pop())
                            if not (isinstance(t, int) and w < 1):
                                pe.wait_ge(row_done, w)
                            for r in range(TILES):
                                mm = nc.tensor.matmul(ps_idx[:, r * P:(r + 1) * P],
                                                      idx16[1 - h][:, r:r + 1].to_broadcast([P, P]),
                                                      id16[:, :], start=True, stop=True)
                            mm.then_inc(idx_spread, 1)

            walk(pe, pair, gn)

        @block.vector
        def _(dve):
            v = nc.vector
            steps = [0]

            def link(ins):
                steps[0] += 1
                ins.then_inc(su_dve, 1)
                dve.wait_ge(su_dve, steps[0])

            dve.wait_ge(in_w, 16)
            link(v.tensor_reduce(small[:, 4:5], w_nat.rearrange("p a b -> p (a b)"), AX.X, ALU.max,
                                 apply_absolute_value=True))
            dve.wait_ge(in_e, 16)
            link(v.tensor_reduce(small[:, 5:6], e_nat.rearrange("p a b -> p (a b)"), AX.X, ALU.max,
                                 apply_absolute_value=True))
            link(v.tensor_copy(small[:, 8:9], small[:, 5:6]))
            assert steps[0] == SU_EMAX
            dve.wait_ge(su_pool, 1)
            link(v.tensor_copy(small[:, 5:6], small[:, 9:10]))
            link(v.tensor_scalar(small[:, 4:6], small[:, 4:6], 2.0 ** -100, 2.0 ** 100, ALU.max, ALU.min))
            link(v.tensor_scalar(small[:, 10:12].bitcast(I32), small[:, 4:6].bitcast(I32), 0x7F800000,
                                 None, ALU.bitwise_and))
            link(v.reciprocal(small[:, 6:8], small[:, 10:12]))
            link(v.tensor_scalar(small[:, 6:8], small[:, 6:8], WS, None, ALU.mult))
            link(v.tensor_scalar(conv_scale, small[:, 10:11], 1.0 / (WS * ZS), None, ALU.mult))
            link(v.tensor_scalar(neg_conv_scale, conv_scale, -1.0, None, ALU.mult))
            link(v.tensor_scalar(code_scale, small[:, 11:12], 1.0 / WS, None, ALU.mult))
            link(v.tensor_scalar(small[:, 2:3], small[:, 11:12], -0.5 * ZS / WS, None, ALU.mult))
            link(v.tensor_scalar(w_scaled, w_nat.rearrange("p c t -> p t c"), small[:, 6:7], None, ALU.mult))
            f0, f1, f2 = (w_scaled[:, KW * i:KW * i + KW, :] for i in (2, 1, 0))
            seg = [w_seg[:, KW * s:KW * s + KW, :] for s in range(SEGS)]
            link(v.tensor_copy(seg[2], f0))
            link(v.tensor_copy(seg[3], f2))
            link(v.tensor_tensor(f0, f0, f2, ALU.add))
            link(v.tensor_tensor(seg[0], f0, f1, ALU.add))
            link(v.tensor_tensor(seg[1], f0, f1, ALU.subtract))
            link(v.tensor_scalar(w_seg[:, 0:2 * KW, :], w_seg[:, 0:2 * KW, :], 0.5, None, ALU.mult))
            link(v.tensor_copy(w_hi, w_seg))
            link(v.tensor_tensor(w_lo, w_seg, w_hi, ALU.subtract))
            link(v.tensor_scalar(e_sc, e_nat, small[:, 7:8], None, ALU.mult))
            link(v.tensor_copy(eR[:, 0], e_sc))
            link(v.tensor_tensor(eR[:, 1], e_sc, eR[:, 0], ALU.subtract))
            link(v.tensor_tensor(e_nat, e_sc, e_sc, ALU.mult))
            link(v.tensor_reduce(small[:, 12:16], e_nat, AX.X, ALU.add))
            dve.wait_ge(in_const, 16)
            for b in range(BLOCKS):
                link(v.tensor_scalar(diag[:, b, :], cst[:, C_ID:C_ID + P], small[:, 12 + b:13 + b],
                                     None, ALU.mult))
            link(v.memset(ones, 1.0))
            link(v.memset(best[0][:, :], 3.0e38))
            link(v.memset(best[1][:, :], 3.0e38))
            link(v.tensor_copy(id16[:, :], cst[:, C_ID:C_ID + P]))
            assert steps[0] == SU_SPLIT
            n = 0
            for tap in range(SEGS * KW):
                for part in range(2):
                    dve.wait_ge(su_pe, n + 1)
                    v.tensor_copy(wT[:, part, tap, :], ps_t16[n % 2]
                                  ).then_inc(su_dve, 1)
                    n += 1
            for b in range(BLOCKS):
                for part in range(2):
                    dve.wait_ge(su_pe, n + 1)
                    v.tensor_copy(eT[:, part, b * P:(b + 1) * P], ps_t16[n % 2]
                                  ).then_inc(su_dve, 1)
                    n += 1
            dve.wait_ge(su_pe, n + 1)
            v.tensor_scalar(code_bias[:, :], ps_score[0][:, :], small[:, 2:3], None,
                            ALU.mult).then_inc(su_dve, 1)
            dve.wait_ge(su_dve, SU_DONE)

            def gn(k, m, t):
                turn = gn_turn(k, m)
                at = [0]

                def link(ins):
                    at[0] += 1
                    ins.then_inc(gn_dve, 1)
                    hold(dve, gn_dve, GN_DVE * turn + at[0])

                hold(dve, stat_done[k], 2 * PPI * (m + 1))
                link(v.tensor_reduce(gt[:, 0:2], stat[k][:, :, :, 0], AX.X, ALU.add))
                link(v.tensor_scalar(gt[:, 0:2], gt[:, 0:2], 1.0 / (H * W), None, ALU.mult))
                link(v.tensor_tensor(gt[:, 2:3], gt[:, 0:1], gt[:, 0:1], ALU.mult))
                link(v.tensor_tensor(gt[:, 1:2], gt[:, 1:2], gt[:, 2:3], ALU.subtract))
                link(v.tensor_tensor(gt[:, 0:1], gt[:, 0:1], neg_shift[k][:, :], ALU.subtract))
                assert at[0] == GN_MEANS
                hold(dve, gn_pe, 2 * turn + 1)
                link(v.tensor_copy(gt[:, 8:10], ps_gn[:, 0:2]))
                link(v.tensor_tensor(gt[:, 3:4], gt[:, 0:1], gt[:, 8:9], ALU.subtract))
                link(v.tensor_tensor(gt[:, 4:5], gt[:, 3:4], gt[:, 3:4], ALU.mult))
                assert at[0] == GN_DIST
                hold(dve, gn_pe, 2 * turn + 2)
                link(v.scalar_tensor_tensor(gt[:, 5:6], ps_gn[:, 2:3], EPS, gt[:, 9:10],
                                            ALU.add, ALU.add))
                assert at[0] == GN_VAR
                hold(dve, gn_act, turn + 1)
                link(v.reciprocal(gt[:, 7:8], gt[:, 6:7]))
                link(v.tensor_tensor(gt[:, 10:11], gt[:, 7:8], gt[:, 7:8], ALU.mult))
                link(v.tensor_tensor(gt[:, 11:12], gt[:, 10:11], gt[:, 5:6], ALU.mult))
                link(v.tensor_scalar(gt[:, 12:13], gt[:, 11:12], -0.5, 1.5, ALU.mult, ALU.add))
                link(v.tensor_tensor(gt[:, 13:14], gt[:, 12:13], gt[:, 7:8], ALU.mult))
                if k == 2:
                    link(v.tensor_copy(neg_shift[2][:, :], next_shift[:, :]))
                else:
                    to = neg_shift[2] if isinstance(m, int) and m == 0 else next_shift
                    link(v.tensor_scalar(to[:, :], gt[:, 0:1], -1.0, None, ALU.mult))
                if not (isinstance(m, int) and m == 0):
                    if k == 1:
                        hold(dve, zb_done, 3 * PPI * m)
                    else:
                        hold(dve, z32v_done, CPI * m)
                link(v.tensor_scalar(gn_ab[k][:, 0:1], gt[:, 13:14], ZS, None, ALU.mult))
                assert at[0] == GN_DVE
                v.scalar_tensor_tensor(gn_ab[k][:, 1:2], gt[:, 8:9], -1.0, gn_ab[k][:, 0:1],
                                       ALU.mult, ALU.mult).then_inc(gn_ready[k], 1)

            def pair(t, on, first=False):
                for h in range(2):
                    c = 2 * (t - L_VQ) + h
                    w = c - 1

                    def top(q):
                        if "vq" not in on:
                            return
                        hold(dve, score_done, TILES * c + q + 1)
                        if not (isinstance(t, int) and TILES * c + q < 2):
                            hold(dve, place_done, TILES * c + q - 1)
                        v.tensor_tensor_reduce(scores[q % 2][:, :], ps_score[q % 2][:, :],
                                               code_bias[:, :], 1.0, -3.0e38, ALU.add, ALU.max,
                                               best[q % 2][:, 0:1]).then_inc(best_done, 1)

                    def find(c, q, h):
                        hold(dve, best_done, TILES * c + q + 1)
                        v.max_index(place[h][:, q, :], best[q % 2][:, :],
                                    scores[q % 2][:, :]).then_inc(place_done, 1)

                    def add(p, s, e, scale, step):
                        if step > 2:
                            hold(dve, x1_done, 4 * p + step - 2)
                        v.scalar_tensor_tensor(rows(p, e), couples(ps_m[s]), scale, rows(p, e),
                                               ALU.mult, ALU.add).then_inc(x1_done, 1)

                    top(0)
                    if f"idx{h}" in on:
                        find(w, TILES - 1, 1 - h)
                    if "end" in on and h == 0:
                        hold(dve, seg_done, SEGS * t)
                        add(t - 1, 3, 1, neg_conv_scale, 4)
                    if "conv" in on and h == 1:
                        hold(dve, seg_done, SEGS * t + 2)
                        hold(dve, xm_done, 2 * (t + 1))
                        add(t, 1, 0, conv_scale, 1)
                        add(t, 1, 1, neg_conv_scale, 2)
                    if f"idx{h}" in on:
                        hold(dve, place_done, TILES * (w + 1))
                        if not (isinstance(t, int) and w < 2):
                            hold(dve, idx_spread, w - 1)
                        v.tensor_copy(idx16[1 - h][:, :], place[1 - h][:, :, 0]).then_inc(idx_done, 1)
                    top(1)
                    if "vq" in on:
                        find(c, 0, h)
                    if f"out{h}" in on:
                        hold(dve, code_done, w)
                        y = slot(t - L_OUT, h)
                        v.scalar_tensor_tensor(y, ps_code[:, :], code_scale, y,
                                               ALU.mult, ALU.add).then_inc(out_done, 1)
                    top(2)
                    if "vq" in on:
                        find(c, 1, h)
                    if f"idx{h}" in on:
                        hold(dve, row_done, w + 1)
                        if not (isinstance(t, int) and w < 1):
                            hold(dve, code_done, w)
                        for b in range(BLOCKS):
                            last = v.tensor_scalar(onehot[:, b, :], idx_row[1 - h][:, :],
                                                   cst[:, C_CODE + b:C_CODE + b + 1], None,
                                                   ALU.is_equal)
                        last.then_inc(onehot_done, 1)
                    top(3)
                    if "vq" in on:
                        find(c, 2, h)
                    if "conv" in on and h == 1:
                        hold(dve, seg_done, SEGS * t + 3)
                        add(t, 2, 0, conv_scale, 3)

            walk(dve, pair, gn)


SU_EMAX = 3
SU_SPLIT = 34
SU_DONE = SU_SPLIT + 2 * (SEGS * KW + BLOCKS) + 1


def walk_loads(sp, pair, setup_over):
    with sp.Fori(0, L_STAT) as i:
        pair(i - L_STAT, {"stats1"})
    setup_over()
    with sp.Fori(0, L_OUT) as t:
        pair(t, {"stats1"})
    pair(L_OUT, {"stats1", "out0", "out1"})
    pair(L_OUT + 1, {"stats1", "out0", "out1", "reuse"})
    with sp.Fori(L_OUT + 2, PAIRS - L_LOAD) as t:
        pair(t, {"stats1", "out0", "out1", "reuse"})
    with sp.Fori(PAIRS - L_LOAD, PAIRS + L_OUT) as t:
        pair(t, {"out0", "out1"})


def kernel(x, L0_conv_weight, L1_conv_embedding):
    import concourse.bacc as bacc
    from concourse.bass_utils import run_bass_kernel_spmd

    nc = bacc.Bacc("TRN2", target_bir_lowering=False, num_devices=1)
    arrays, args = {}, []
    for name, a in (("x", x), ("weight", L0_conv_weight), ("embedding", L1_conv_embedding),
                    ("const", constants())):
        a = np.ascontiguousarray(a)
        arrays[f"in_{name}"] = a
        args.append(nc.dram_tensor(f"in_{name}", a.shape, mybir.dt.from_np(a.dtype),
                                   kind="ExternalInput").ap())
    args.append(nc.dram_tensor("out_0", x.shape, F32, kind="ExternalOutput").ap())
    program(nc, *args)
    r = run_bass_kernel_spmd(nc, [arrays], core_ids=[0])
    return r.results[0]["out_0"]
```

```python
from contextlib import ExitStack

import numpy as np

import concourse.bass as bass
from concourse import mybir

F32 = mybir.dt.float32
F16 = mybir.dt.float16
I32 = mybir.dt.int32
U32 = mybir.dt.uint32
ALU = mybir.AluOpType
ACT = mybir.ActivationFunctionType
AX = mybir.AxisListType

P = 128
IMGS, H, W = 16, 128, 128
CODES = 512
BLOCKS = CODES // P
TAPS = 9
SEGS = 4
KW = 3
PROW = 2
COUPLES = 2 * PROW
ROWS = 4
CH = ROWS * W
TILES = CH // P
CPI = H // ROWS
PPI = CPI // 2
PAIRS = IMGS * PPI
HALO = 2
GROUP = 4
EPS = 1e-5

L_STAT = PPI + 1
L_LOAD = L_STAT + 1
L_VQZ = PPI + 1
L_VQ = L_VQZ + 1
L_OUT = L_VQ + 1
RING = L_LOAD + L_VQ + 2
EARLY = L_LOAD

ZS = 64.0
WS = 256.0

C_ID, C_GRP, C_CODE = 0, P, 2 * P
C_ALL = 2 * P + BLOCKS


def constants():
    c = np.zeros((P, C_ALL), np.float32)
    c[:, C_ID:C_ID + P] = np.eye(P)
    c[:, C_GRP:C_GRP + P] = np.kron(np.eye(P // GROUP), np.full((GROUP, GROUP), 1.0 / GROUP))
    c[:, C_CODE:C_CODE + BLOCKS] = np.arange(P)[:, None] + P * np.arange(BLOCKS)[None, :]
    return c


def walk(eng, pair):
    def span(lo, hi, on):
        with eng.Fori(lo, hi) as t:
            pair(t, on)

    front = {"stats1", "no_vq"}
    convz = front | {"convz"}
    conv = convz | {"conv", "end"}
    full = conv - {"no_vq"} | {"vqz", "vq", "idx0", "idx1", "out0", "out1"}
    pair(-L_STAT, front)
    with eng.Fori(1, L_STAT // 2) as i:
        for odd in (1, 0):
            pair(2 * i - odd - L_STAT, front | {"early", "odd" if odd else "even"})
    pair(-2, front, gn=(1, 0))
    pair(-1, convz, first=0)
    pair(0, conv - {"end"})
    pair(1, conv)
    span(2, PPI - 2, conv)
    pair(PPI - 2, conv, gn=(1, 1))
    pair(PPI - 1, conv, first=1)
    pair(PPI, conv)
    pair(PPI + 1, conv | {"vqz"}, gn=(2, 0))
    pair(PPI + 2, conv - {"no_vq"} | {"vqz", "vq", "idx1"})
    pair(PPI + 3, full)
    span(PPI + 4, 2 * PPI - 2, full)
    with eng.Fori(1, IMGS - 2) as j:
        pair(PPI * j + PPI - 2, full, gn=(1, j + 1))
        pair(PPI * j + PPI - 1, full, first=j + 1)
        pair(PPI * j + PPI, full)
        pair(PPI * j + PPI + 1, full, gn=(2, j))
        with eng.Fori(PPI * j + PPI + 2, PPI * j + 2 * PPI - 2) as t:
            pair(t, full)
    late = full - {"stats1"}
    last = PAIRS - PPI
    pair(last - 2, full, gn=(1, IMGS - 1))
    pair(last - 1, late, first=IMGS - 1)
    pair(last, late)
    pair(last + 1, late, gn=(2, IMGS - 2))
    span(last + 2, PAIRS - 1, late)
    pair(PAIRS - 1, late - {"convz"})
    tail = {"no_conv", "vqz", "vq", "idx0", "idx1", "out0", "out1"}
    pair(PAIRS, tail | {"end"})
    pair(PAIRS + 1, tail, gn=(2, IMGS - 1))
    span(PAIRS + 2, PAIRS + L_VQZ, tail)
    pair(PAIRS + L_VQZ, tail - {"vqz"})
    pair(PAIRS + L_VQ, {"no_conv", "idx0", "out0", "out1"})


def program(nc, x, weight, embedding, const, out, idx_line):
    ctx = ExitStack()
    with ctx:
        def sb(name, shape, dt=F32):
            return ctx.enter_context(nc.sbuf_tensor(name, shape, dt))

        def pb(name, shape, dt=F32):
            return ctx.enter_context(nc.psum_tensor(name, shape, dt))

        def sem(name):
            return ctx.enter_context(nc.semaphore(name))

        ring = sb("ring", [P, RING, COUPLES, 2, W])
        cst = sb("cst", [P, C_ALL])
        id16 = sb("id16", [P, P], F16)
        wT = sb("wT", [P, 2, SEGS * KW, P], F16)
        eT = sb("eT", [P, 2, CODES], F16)
        eR = sb("eR", [P, 2, BLOCKS, P], F16)
        code_bias = sb("code_bias", [P, CODES])
        zb = sb("zb", [P, 2 * COUPLES + HALO, W + HALO])
        t32 = [sb(f"t32{k}", [P, COUPLES, W + HALO]) for k in range(2)]
        th = sb("th", [P, 2, SEGS, COUPLES, W + HALO], F16)
        m1 = sb("m1", [P, COUPLES, W])
        junk = sb("junk", [P, 2 * CH], mybir.dt.bfloat16)
        z32v = sb("z32v", [P, CH])
        zv = [sb(f"zv{h}", [P, 2, CH], F16) for h in range(2)]
        scores = [sb(f"scores{q}", [P, CODES]) for q in range(TILES)]
        best = [sb(f"best{q}", [P, 8]) for q in range(TILES)]
        place = [sb(f"place{h}", [P, TILES, 8], U32) for h in range(2)]
        idx16 = [sb(f"idx16{h}", [P, TILES], F16) for h in range(2)]
        idx_row = [sb(f"idx_row{h}", [P, CH], F16) for h in range(2)]
        onehot = sb("onehot", [P, BLOCKS, CH], F16)
        stat = [None, sb("stat1", [P, 2, PPI, 1]), sb("stat2", [P, 2, PPI, 1])]
        neg_shift = [None, sb("neg_shift1", [P, 1]), sb("neg_shift2", [P, 1])]
        next_shift = sb("next_shift", [P, 1])
        gn_ab = [None, sb("gn_ab1", [P, 2]), sb("gn_ab2", [P, 2])]
        gt = sb("gt", [P, 16])
        small = sb("small", [P, 16])
        conv_scale = small[:, 0:1]
        code_scale = small[:, 1:2]
        neg_conv_scale = small[:, 3:4]

        def scratch(slot, shape):
            n = int(np.prod(shape))
            names = "abc"[:len(shape)]
            flat = ring[:, slot:slot + 2].rearrange("p s c e w -> p (s c e w)")[:, 0:n]
            return flat.rearrange(f"p ({' '.join(names)}) -> p {' '.join(names)}",
                                  **{k: v for k, v in zip(names[1:], shape[1:])})

        S0 = L_LOAD + 1
        w_nat = scratch(S0, [P, TAPS])
        w_scaled = scratch(S0 + 2, [TAPS, P])
        w_hi = scratch(S0 + 4, [SEGS * KW, P // 2]).bitcast(F16)
        w_lo = scratch(S0 + 6, [SEGS * KW, P // 2]).bitcast(F16)
        w_seg = scratch(S0 + 16, [SEGS * KW, P])
        e_nat = scratch(S0 + 8, [BLOCKS, P])
        e_sc = scratch(S0 + 10, [BLOCKS, P])
        diag = scratch(S0 + 12, [BLOCKS, P])
        ones = scratch(S0 + 14, [P])

        ps_m = [pb(f"ps_m{s}", [P, CH]) for s in range(SEGS)]
        ps_score = [pb(f"ps_score{k}", [P, CODES]) for k in range(2)]
        ps_gn = pb("ps_gn", [P, CH])
        ps_code = pb("ps_code", [P, CH])
        ps_t16 = [ps[:, 0:P // 2].bitcast(F16) for ps in (ps_gn, ps_code)]

        loaded = [sem(f"loaded{h}") for h in range(2)]
        stored = [sem(f"stored{h}") for h in range(2)]
        stat_done = [None, sem("stat1_done"), sem("stat2_done")]
        zb_done = sem("zb_done")
        t32_done = sem("t32_done")
        thi_done = sem("thi_done")
        th_done = sem("th_done")
        seg_done = sem("seg_done")
        m1_done = sem("m1_done")
        xm_done = sem("xm_done")
        x1_done = sem("x1_done")
        shift_done = sem("shift_done")
        z32v_done = sem("z32v_done")
        zhv_done = sem("zhv_done")
        zv_done = sem("zv_done")
        score_done = sem("score_done")
        best_done = sem("best_done")
        place_done = sem("place_done")
        idx_done = sem("idx_done")
        idx_saved = sem("idx_saved")
        row_done = sem("row_done")
        onehot_done = sem("onehot_done")
        code_done = sem("code_done")
        code_scaled = sem("code_scaled")
        out_done = sem("out_done")
        gn_dve = sem("gn_dve")
        gn_pe = sem("gn_pe")
        gn_act = sem("gn_act")
        gn_ready = [None, sem("gn_ready1"), sem("gn_ready2")]
        in_const, in_w, in_e = sem("in_const"), sem("in_w"), sem("in_e")
        su_dve = sem("su_dve")
        su_pe = sem("su_pe")
        su_pool = sem("su_pool")

        GN_DVE = 13
        GN_MEANS, GN_DIST, GN_VAR = 4, 7, 8
        NO_CONV = 2 * (PAIRS - L_VQ) - 2
        xp = x.rearrange("b c (k r) w -> c b k (r w)", r=2 * ROWS)
        xv = x.rearrange("b c (k h r) w -> c b k h (r w)", h=2, r=ROWS)
        ov = out.rearrange("b c (k h r) w -> c b k h (r w)", h=2, r=ROWS)

        def pixels(pair):
            return ring[:, pair % RING, :, :, :].rearrange("p c e w -> p (c e w)")

        def slot(pair, h):
            return pixels(pair)[:, h * CH:(h + 1) * CH]

        def rows(pair, e):
            return ring[:, pair % RING, :, e, :]

        d = [zb[:, 2 * (i // 2):2 * (i // 2) + 2 * COUPLES, :].rearrange(
            "p (k e) w -> p k e w", e=2)[:, :, i % 2, :] for i in range(4)]
        seg_input = [(d[1], d[2], ALU.add), (d[2], d[1], ALU.subtract),
                     (d[0], d[2], ALU.subtract), (d[1], d[3], ALU.subtract)]

        def couples(ps):
            return ps[:, :].rearrange("p (k w) -> p k w", w=W)

        code_pixels = ps_code[:, :].rearrange("p (w r) -> p r w", r=TILES)

        def gn_turn(k, m):
            if isinstance(m, int) and (k, m) in ((1, 0), (2, IMGS - 1)):
                return 0 if k == 1 else 2 * m + 1
            return 2 * m - 1 if k == 1 else 2 * m + 2

        def gn_half(gn):
            return None if gn is None else 2 - gn[0]

        def hold(eng, s, value):
            if not isinstance(value, int):
                value = eng.to_reg(value)
                eng.wait_ge(in_const, 16)
            eng.wait_ge(s, value)

        def lo(eng, t, s):
            hold(eng, thi_done, SEGS * (t + 1) + s + 1)
            eng.tensor_tensor(th[:, 1, s, :, :], t32[s % 2][:, :, :], th[:, 0, s, :, :],
                              ALU.subtract).then_inc(th_done, 1)

        def add_m1(eng, t, e):
            hold(eng, m1_done, t + 1)
            eng.tensor_tensor(rows(t, e), rows(t, e), m1[:, :, :], ALU.add).then_inc(xm_done, 1)

        block = ctx.enter_context(nc.Block())

        @block.sync
        def _(sp):
            sp.dma_start(cst[:, :], const).then_inc(in_const, 16)
            sp.dma_start(w_nat.rearrange("p a b -> p (a b)"),
                         weight.rearrange("o c i j -> o (c i j)")).then_inc(in_w, 16)
            sp.dma_start(e_nat, embedding.rearrange("(b k) c -> k b c", k=P)).then_inc(in_e, 16)

            def load_early(p, odd):
                if not (isinstance(p, int) and p < 2):
                    sp.wait_ge(loaded[odd], 16 * (p // 2))
                sp.dma_start(pixels(p), xp[:, p // PPI, p % PPI, :]).then_inc(loaded[odd], 16)

            def load(p, h):
                sp.wait_ge(loaded[h], 16 * (p - EARLY // 2))
                sp.dma_start(slot(p, h), xv[:, p // PPI, p % PPI, h, :]).then_inc(loaded[h], 16)

            def store(p, h):
                values = 2 * p + h + 1, 16 * p
                if not isinstance(p, int):
                    values = [sp.to_reg(n) for n in values]
                sp.wait_ge(out_done, values[0])
                if not (isinstance(p, int) and p == 0):
                    sp.wait_ge(stored[h], values[1])
                sp.dma_start(ov[:, p // PPI, p % PPI, h, :], slot(p, h)).then_inc(stored[h], 16)

            def spread(w, h):
                values = 16 * w, w + 1, 16 * (w + 1), w - 1
                if not isinstance(w, int):
                    values = [sp.to_reg(n) for n in values]
                if not (isinstance(w, int) and w < 1):
                    sp.wait_ge(row_done, values[0])
                sp.wait_ge(idx_done, values[1])
                sp.dma_start(idx_line.rearrange("(p r) -> p r", r=TILES),
                             idx16[1 - h][:, :]).then_inc(idx_saved, 16)
                if not (isinstance(w, int) and w < 2):
                    sp.wait_ge(onehot_done, values[3])
                sp.wait_ge(idx_saved, values[2])
                sp.dma_start(idx_row[1 - h][:, :], idx_line.partition_broadcast(P)).then_inc(row_done, 16)

            assert EARLY % 2 == 0
            load_early(0, 0)
            load_early(1, 1)
            with sp.Fori(1, EARLY // 2) as i:
                for odd in range(2):
                    load_early(2 * i + odd, odd)

            def pair(t, on, first=None, gn=None):
                for h in range(2):
                    if "stats1" in on and not (isinstance(t, int) and t + L_LOAD >= PAIRS):
                        if "reuse" in on:
                            sp.wait_ge(stored[h], 16 * (t + L_LOAD - RING + 1))
                        load(t + L_LOAD, h)
                    if f"idx{h}" in on:
                        spread(2 * (t - L_VQ) + h - 1, h)
                    if f"out{h}" in on:
                        store(t - L_OUT, h)

            walk_loads(sp, pair, lambda: sp.wait_ge(su_dve, SU_DONE))
            for h in range(2):
                sp.wait_ge(stored[h], 16 * PAIRS)

        @block.scalar
        def _(act):
            def gn_root(gn):
                hold(act, gn_dve, GN_DVE * gn_turn(*gn) + GN_VAR)
                nc.scalar.activation(gt[:, 11:12], gt[:, 10:11], ACT.Sqrt).then_inc(gn_act, 1)

            def shift1(p):
                nc.scalar.mul(neg_shift[1][:, :], pixels(p)[:, 0:1], -1.0).then_inc(shift_done, 1)
                hold(act, shift_done, p // PPI + 1)

            def stats(k, p, last, which=(0, 1)):
                for k0, p0 in last:
                    hold(act, stat_done[k0], 2 * (p0 + 1))
                for n in which:
                    if n == 1:
                        hold(act, stat_done[k], 2 * p + 1)
                    nc.scalar.activation(junk[:, :], pixels(p), (ACT.Identity, ACT.Square)[n],
                                         bias=neg_shift[k][:, :], accum_out=stat[k][:, n, p % PPI, :]
                                         ).then_inc(stat_done[k], 1)

            def wait_loaded(p, on):
                if isinstance(p, int) and p < EARLY:
                    hold(act, loaded[p % 2], 16 * (p // 2 + 1))
                elif "early" in on:
                    hold(act, loaded["odd" in on], 16 * (p // 2 + 1))
                else:
                    for h in range(2):
                        hold(act, loaded[h], 16 * (p - EARLY // 2 + 1))

            scalars = dict(bias=gn_ab[1][:, 1:2], scale=gn_ab[1][:, 0:1])

            def z_halo(t, first):
                p = t + 1
                if first is not None:
                    hold(act, gn_ready[1], p // PPI + 1)
                if not (isinstance(t, int) and p == 0):
                    hold(act, t32_done, SEGS * p)
                    hold(act, zb_done, 3 * p)
                if first is not None:
                    last = ring[:, (p + PPI - 1) % RING, COUPLES - 1, :, :]
                    nc.scalar.activation(zb[:, 0:HALO, HALO:], last, ACT.Identity,
                                         **scalars).then_inc(zb_done, 1)
                else:
                    nc.scalar.copy(zb[:, 0:HALO, :], zb[:, 2 * COUPLES:, :]).then_inc(zb_done, 1)

            def z_rows(t, first):
                p = t + 1
                hold(act, zb_done, 3 * p + 1)
                nc.scalar.activation(zb[:, HALO:, HALO:],
                                     pixels(p).rearrange("p (r w) -> p r w", w=W), ACT.Identity,
                                     **scalars).then_inc(zb_done, 1)
                hold(act, zb_done, 3 * p + 2)
                r0 = HALO if first is None else 0
                nc.scalar.copy(zb[:, r0:, 0:HALO], zb[:, r0:, W:]).then_inc(zb_done, 1)

            def hi(t, s):
                n = SEGS * (t + 1) + s
                hold(act, t32_done, n + 1)
                if not (isinstance(t, int) and t < 0):
                    hold(act, seg_done, n - SEGS + 1)
                nc.scalar.copy(th[:, 0, s, :, :], t32[s % 2][:, :, :]).then_inc(thi_done, 1)

            def z_vq(t, h):
                c = 2 * (t - L_VQZ) + h
                hold(act, gn_ready[2], (t - L_VQZ) // PPI + 1)
                if not (isinstance(t, int) and c < 1):
                    hold(act, zv_done, c)
                nc.scalar.activation(z32v[:, :], slot(t - L_VQZ, h), ACT.Identity,
                                     bias=gn_ab[2][:, 1:2], scale=gn_ab[2][:, 0:1]
                                     ).then_inc(z32v_done, 1)

            def hi_vq(t, h):
                c = 2 * (t - L_VQZ) + h
                if not (isinstance(t, int) and c < 2):
                    hold(act, score_done, TILES * (c - 1))
                hold(act, z32v_done, c + 1)
                nc.scalar.copy(zv[h][:, 0, :], z32v[:, :]).then_inc(zhv_done, 1)

            def scale_codes(t, h):
                y = 2 * (t - L_VQ) + h - 2
                hold(act, code_done, y + 1)
                hold(act, xm_done, 2 * PAIRS)
                hold(act, out_done, y)
                nc.scalar.mul(m1[:, :, :], code_pixels, code_scale).then_inc(code_scaled, 1)

            def pair(t, on, first=None, gn=None):
                k2 = gn is not None and gn[0] == 2
                if "convz" in on:
                    z_halo(t, first)
                if "convz" in on:
                    z_rows(t, first)
                if "no_conv" in on and "out0" in on and (k2 or "vqz" not in on):
                    scale_codes(t, 0)
                if "conv" in on:
                    hold(act, seg_done, SEGS * t + 1)
                    if not (isinstance(t, int) and t < 1):
                        hold(act, xm_done, 2 * t)
                    nc.scalar.mul(m1[:, :, :], couples(ps_m[0]), conv_scale).then_inc(m1_done, 1)
                alone = "no_vq" in on and gn is None and "vqz" not in on
                if "stats1" in on:
                    p = t + L_STAT
                    wait_loaded(p, on)
                    if first is not None:
                        shift1(p)
                    if "end" in on and not (isinstance(t, int) and t < 2):
                        before = [(2, t - 2)]
                    else:
                        before = [] if isinstance(p, int) and p == 0 else [(1, p - 1)]
                if alone:
                    if "stats1" in on:
                        stats(1, p, before, (0,))
                    if "convz" in on:
                        hi(t, 0)
                    if "stats1" in on:
                        stats(1, p, [], (1,))
                else:
                    if "convz" in on:
                        hi(t, 0)
                    if "stats1" in on:
                        stats(1, p, before)
                if "convz" in on:
                    hi(t, 1)
                if "vqz" in on and not k2:
                    z_vq(t, 0)
                    hi_vq(t, 0)
                if "no_conv" in on and "vqz" in on and not k2:
                    scale_codes(t, 0)
                if k2:
                    gn_root(gn)
                if "vqz" in on and k2:
                    z_vq(t, 0)
                    hi_vq(t, 0)
                if "end" in on and alone:
                    hold(act, x1_done, 4 * t)
                    stats(2, t - 1, [(1, t + L_STAT)], (0,))
                if "convz" in on:
                    hi(t, 2)
                if "end" in on and alone:
                    stats(2, t - 1, [], (1,))
                if "end" in on and not alone:
                    hold(act, x1_done, 4 * t)
                    if "vqz" in on:
                        hold(act, gn_ready[2], (t - 1) // PPI)
                    stats(2, t - 1, [(1, t + L_STAT)] if "stats1" in on else [(2, t - 2)])
                if "vqz" in on:
                    z_vq(t, 1)
                    hi_vq(t, 1)
                if "no_conv" in on and "out1" in on:
                    scale_codes(t, 1)
                if "convz" in on:
                    hi(t, 3)
                if gn is not None and gn[0] == 1:
                    gn_root(gn)

            wait_loaded(0, ())
            shift1(0)
            walk(act, pair)

        @block.gpsimd
        def _(pool):
            pool.wait_ge(su_dve, SU_EMAX)
            nc.gpsimd.partition_all_reduce(small[:, 9:10], small[:, 8:9], P,
                                           bass.bass_isa.ReduceOp.max).then_inc(su_pool, 1)

            def transform(t, s):
                p = t + 1
                if s == 0:
                    hold(pool, zb_done, 3 * (p + 1))
                n = SEGS * p + s
                if not (isinstance(n, int) and n < 2):
                    hold(pool, th_done, n - 1)
                a, b, op = seg_input[s]
                nc.gpsimd.tensor_tensor(t32[s % 2][:, :, :], a, b, op).then_inc(t32_done, 1)

            def lo_vq(t, h):
                hold(pool, zhv_done, 2 * (t - L_VQZ) + h + 1)
                nc.gpsimd.tensor_tensor(zv[h][:, 1, :], z32v[:, :], zv[h][:, 0, :],
                                        ALU.subtract).then_inc(zv_done, 1)

            def add_codes(t, h):
                y = 2 * (t - L_VQ) + h - 2
                hold(pool, code_scaled, y - NO_CONV + 1)
                nc.gpsimd.tensor_tensor(slot(t - L_OUT, h), slot(t - L_OUT, h), m1[:, :, :].rearrange(
                    "p k w -> p (k w)"), ALU.add).then_inc(out_done, 1)

            def pair(t, on, first=None, gn=None):
                if "no_vq" in on:
                    if "convz" in on:
                        for s in range(SEGS):
                            transform(t, s)
                    if "vqz" in on:
                        for h in range(2):
                            lo_vq(t, h)
                    return
                k2 = gn is not None and gn[0] == 2
                if "no_conv" in on:
                    if k2:
                        add_codes(t, 0)
                    if "vqz" in on:
                        lo_vq(t, 0)
                    if not k2:
                        add_codes(t, 0)
                    if "vqz" in on:
                        lo_vq(t, 1)
                    add_codes(t, 1)
                    return
                if "convz" in on:
                    transform(t, 0)
                    transform(t, 1)
                    lo(pool, t, 0)
                if "conv" in on:
                    for e in range(2):
                        add_m1(pool, t, e)
                if "convz" in on:
                    transform(t, 2)
                    lo(pool, t, 1)
                if "vqz" in on and not k2:
                    lo_vq(t, 0)
                if "convz" in on:
                    transform(t, 3)
                if "vqz" in on and k2:
                    lo_vq(t, 0)
                if "convz" in on:
                    lo(pool, t, 2)
                if "vqz" in on:
                    lo_vq(t, 1)
                if "convz" in on:
                    lo(pool, t, 3)

            walk(pool, pair)

        @block.tensor
        def _(pe):
            pe.wait_ge(su_dve, SU_SPLIT)
            n = 0
            for tap in range(SEGS * KW):
                for part, src in enumerate((w_hi, w_lo)):
                    if n >= 2:
                        pe.wait_ge(su_dve, SU_SPLIT + n - 1)
                    nc.tensor.transpose(ps_t16[n % 2], src[:, tap, :],
                                        id16[:, :]).then_inc(su_pe, 1)
                    n += 1
            for b in range(BLOCKS):
                for part in range(2):
                    pe.wait_ge(su_dve, SU_SPLIT + n - 1)
                    nc.tensor.transpose(ps_t16[n % 2], eR[:, part, b, :],
                                        id16[:, :]).then_inc(su_pe, 1)
                    n += 1
            for b in range(BLOCKS):
                mm = nc.tensor.matmul(ps_score[0][:, b * P:(b + 1) * P], ones, diag[:, b, :],
                                      start=True, stop=True)
            mm.then_inc(su_pe, 1)
            pe.wait_ge(su_dve, SU_DONE)

            def gn_sums(gn, step):
                turn = gn_turn(*gn)
                grp = cst[:, C_GRP:C_GRP + P]
                if step == 0:
                    pe.wait_ge(gn_dve, GN_DVE * turn + GN_MEANS)
                    nc.tensor.matmul(ps_gn[:, 0:2], grp, gt[:, 2:4],
                                     start=True, stop=True).then_inc(gn_pe, 1)
                else:
                    pe.wait_ge(gn_dve, GN_DVE * turn + GN_DIST)
                    nc.tensor.matmul(ps_gn[:, 2:3], grp, gt[:, 7:8],
                                     start=True, stop=True).then_inc(gn_pe, 1)

            products = [(j, wp, zp) for j in range(KW) for wp, zp in ((0, 0), (1, 0), (0, 1))]

            def segment(t, s, part):
                if part == 0:
                    pe.wait_ge(th_done, SEGS * t + s + 1)
                    if not (isinstance(t, int) and t < 1):
                        if s == 0:
                            pe.wait_ge(m1_done, t)
                        else:
                            pe.wait_ge(x1_done, 4 * (t - 1) + s + 1)
                for n in (range(5), range(5, len(products)))[part]:
                    j, wp, zp = products[n]
                    mm = nc.tensor.matmul(couples(ps_m[s]), wT[:, wp, KW * s + j, :],
                                          th[:, zp, s, :, HALO - j:HALO - j + W],
                                          start=(n == 0), stop=(n == len(products) - 1))
                if part:
                    mm.then_inc(seg_done, 1)

            def pair(t, on, first=None, gn=None):
                for h in range(2):
                    v = 2 * (t - L_VQ) + h
                    w = v - 1
                    for q in range(TILES):
                        if "vq" in on:
                            if q == 0:
                                pe.wait_ge(zv_done, v + 1)
                            if not (isinstance(t, int) and TILES * v + q < 2):
                                pe.wait_ge(best_done, TILES * v + q - 1)
                            tile = slice(q * P, (q + 1) * P)
                            ps = ps_score[q % 2][:, :]
                            nc.tensor.matmul(ps, zv[h][:, 0, tile], eT[:, 0, :], start=True, stop=False)
                            nc.tensor.matmul(ps, zv[h][:, 0, tile], eT[:, 1, :], start=False, stop=False)
                            nc.tensor.matmul(ps, zv[h][:, 1, tile], eT[:, 0, :],
                                             start=False, stop=True).then_inc(score_done, 1)
                        if f"out{h}" in on and q == 3:
                            y = w - 1
                            pe.wait_ge(onehot_done, y + 1)
                            if not (isinstance(t, int) and y < 1):
                                pe.wait_ge(out_done, y)
                            for b in range(BLOCKS):
                                for part in range(2):
                                    mm = nc.tensor.matmul(
                                        ps_code[:, :], eR[:, part, b, :], onehot[:, b, :],
                                        start=(b == 0 and part == 0),
                                        stop=(b == BLOCKS - 1 and part == 1))
                            mm.then_inc(code_done, 1)
                        if "conv" in on:
                            segment(t, 2 * h + q // 2, q % 2)
                        if h == gn_half(gn) and q >= 2:
                            gn_sums(gn, q - 2)

            walk(pe, pair)

        @block.vector
        def _(dve):
            v = nc.vector
            steps = [0]

            def link(ins):
                steps[0] += 1
                ins.then_inc(su_dve, 1)
                dve.wait_ge(su_dve, steps[0])

            dve.wait_ge(in_w, 16)
            link(v.tensor_reduce(small[:, 4:5], w_nat.rearrange("p a b -> p (a b)"), AX.X, ALU.max,
                                 apply_absolute_value=True))
            dve.wait_ge(in_e, 16)
            link(v.tensor_reduce(small[:, 5:6], e_nat.rearrange("p a b -> p (a b)"), AX.X, ALU.max,
                                 apply_absolute_value=True))
            link(v.tensor_copy(small[:, 8:9], small[:, 5:6]))
            assert steps[0] == SU_EMAX
            dve.wait_ge(su_pool, 1)
            link(v.tensor_copy(small[:, 5:6], small[:, 9:10]))
            link(v.tensor_scalar(small[:, 4:6], small[:, 4:6], 2.0 ** -100, 2.0 ** 100, ALU.max, ALU.min))
            link(v.tensor_scalar(small[:, 10:12].bitcast(I32), small[:, 4:6].bitcast(I32), 0x7F800000,
                                 None, ALU.bitwise_and))
            link(v.reciprocal(small[:, 6:8], small[:, 10:12]))
            link(v.tensor_scalar(small[:, 6:8], small[:, 6:8], WS, None, ALU.mult))
            link(v.tensor_scalar(conv_scale, small[:, 10:11], 1.0 / (WS * ZS), None, ALU.mult))
            link(v.tensor_scalar(neg_conv_scale, conv_scale, -1.0, None, ALU.mult))
            link(v.tensor_scalar(code_scale, small[:, 11:12], 1.0 / WS, None, ALU.mult))
            link(v.tensor_scalar(small[:, 2:3], small[:, 11:12], -0.5 * ZS / WS, None, ALU.mult))
            link(v.tensor_scalar(w_scaled, w_nat.rearrange("p c t -> p t c"), small[:, 6:7], None, ALU.mult))
            f0, f1, f2 = (w_scaled[:, KW * i:KW * i + KW, :] for i in (2, 1, 0))
            seg = [w_seg[:, KW * s:KW * s + KW, :] for s in range(SEGS)]
            link(v.tensor_copy(seg[2], f0))
            link(v.tensor_copy(seg[3], f2))
            link(v.tensor_tensor(f0, f0, f2, ALU.add))
            link(v.tensor_tensor(seg[0], f0, f1, ALU.add))
            link(v.tensor_tensor(seg[1], f0, f1, ALU.subtract))
            link(v.tensor_scalar(w_seg[:, 0:2 * KW, :], w_seg[:, 0:2 * KW, :], 0.5, None, ALU.mult))
            link(v.tensor_copy(w_hi, w_seg))
            link(v.tensor_tensor(w_lo, w_seg, w_hi, ALU.subtract))
            link(v.tensor_scalar(e_sc, e_nat, small[:, 7:8], None, ALU.mult))
            link(v.tensor_copy(eR[:, 0], e_sc))
            link(v.tensor_tensor(eR[:, 1], e_sc, eR[:, 0], ALU.subtract))
            link(v.tensor_tensor(e_nat, e_sc, e_sc, ALU.mult))
            link(v.tensor_reduce(small[:, 12:16], e_nat, AX.X, ALU.add))
            dve.wait_ge(in_const, 16)
            for b in range(BLOCKS):
                link(v.tensor_scalar(diag[:, b, :], cst[:, C_ID:C_ID + P], small[:, 12 + b:13 + b],
                                     None, ALU.mult))
            link(v.memset(ones, 1.0))
            for k in range(TILES):
                link(v.memset(best[k][:, :], 3.0e38))
            link(v.tensor_copy(id16[:, :], cst[:, C_ID:C_ID + P]))
            assert steps[0] == SU_SPLIT
            n = 0
            for tap in range(SEGS * KW):
                for part in range(2):
                    dve.wait_ge(su_pe, n + 1)
                    v.tensor_copy(wT[:, part, tap, :], ps_t16[n % 2]
                                  ).then_inc(su_dve, 1)
                    n += 1
            for b in range(BLOCKS):
                for part in range(2):
                    dve.wait_ge(su_pe, n + 1)
                    v.tensor_copy(eT[:, part, b * P:(b + 1) * P], ps_t16[n % 2]
                                  ).then_inc(su_dve, 1)
                    n += 1
            dve.wait_ge(su_pe, n + 1)
            v.tensor_scalar(code_bias[:, :], ps_score[0][:, :], small[:, 2:3], None,
                            ALU.mult).then_inc(su_dve, 1)
            dve.wait_ge(su_dve, SU_DONE)

            def gn_part(gn, part):
                k, m = gn
                turn = gn_turn(k, m)

                def col(n):
                    return gt[:, n:n + 1]

                def after(step):
                    hold(dve, gn_dve, GN_DVE * turn + step)

                if part == "means":
                    hold(dve, stat_done[k], 2 * PPI * (m + 1))
                    v.tensor_reduce(gt[:, 0:2], stat[k][:, :, :, 0], AX.X, ALU.add).then_inc(gn_dve, 1)
                    after(1)
                    v.tensor_scalar(gt[:, 4:6], gt[:, 0:2], 1.0 / (H * W), None,
                                    ALU.mult).then_inc(gn_dve, 1)
                    after(2)
                    v.tensor_tensor(col(2), col(4), neg_shift[k][:, :], ALU.subtract).then_inc(gn_dve, 1)
                    v.scalar_tensor_tensor(col(3), col(4), col(4), col(5), ALU.mult,
                                           ALU.subtract).then_inc(gn_dve, 1)
                elif part == "distance":
                    hold(dve, gn_pe, 2 * turn + 1)
                    v.tensor_copy(gt[:, 8:10], ps_gn[:, 0:2]).then_inc(gn_dve, 1)
                    v.tensor_tensor(col(6), col(2), ps_gn[:, 0:1], ALU.subtract).then_inc(gn_dve, 1)
                    after(6)
                    v.tensor_tensor(col(7), col(6), col(6), ALU.mult).then_inc(gn_dve, 1)
                elif part == "variance":
                    hold(dve, gn_pe, 2 * turn + 2)
                    after(7)
                    v.scalar_tensor_tensor(col(10), ps_gn[:, 2:3], EPS, col(9),
                                           ALU.add, ALU.subtract).then_inc(gn_dve, 1)
                else:
                    hold(dve, gn_act, turn + 1)
                    v.reciprocal(col(12), col(11)).then_inc(gn_dve, 1)
                    after(9)
                    v.scalar_tensor_tensor(col(13), col(12), col(10), col(12), ALU.mult,
                                           ALU.mult).then_inc(gn_dve, 1)
                    after(10)
                    v.tensor_scalar(col(14), col(13), -0.5, 1.5, ALU.mult, ALU.add).then_inc(gn_dve, 1)
                    if k == 2:
                        v.tensor_copy(neg_shift[2][:, :], next_shift[:, :]).then_inc(gn_dve, 1)
                    else:
                        to = neg_shift[2] if isinstance(m, int) and m == 0 else next_shift
                        v.tensor_scalar(to[:, :], col(2), -1.0, None, ALU.mult).then_inc(gn_dve, 1)
                    if not (isinstance(m, int) and m == 0):
                        if k == 1:
                            hold(dve, zb_done, 3 * PPI * m)
                        else:
                            hold(dve, z32v_done, CPI * m)
                    after(12)
                    v.scalar_tensor_tensor(gn_ab[k][:, 0:1], col(14), ZS, col(12), ALU.mult,
                                           ALU.mult).then_inc(gn_dve, 1)
                    after(GN_DVE)
                    v.scalar_tensor_tensor(gn_ab[k][:, 1:2], col(8), -1.0, gn_ab[k][:, 0:1],
                                           ALU.mult, ALU.mult).then_inc(gn_ready[k], 1)

            def pair(t, on, first=None, gn=None):
                for h in range(2):
                    c = 2 * (t - L_VQ) + h
                    w = c - 1

                    def top(q):
                        if "vq" not in on:
                            return
                        hold(dve, score_done, TILES * c + q + 1)
                        if not (isinstance(t, int) and c < 1):
                            hold(dve, place_done, TILES * (c - 1) + q + 1)
                        v.tensor_tensor_reduce(scores[q][:, :], ps_score[q % 2][:, :],
                                               code_bias[:, :], 1.0, -3.0e38, ALU.add, ALU.max,
                                               best[q][:, 0:1]).then_inc(best_done, 1)

                    def find(c, q, h):
                        hold(dve, best_done, TILES * c + q + 1)
                        v.max_index(place[h][:, q, :], best[q][:, :],
                                    scores[q][:, :]).then_inc(place_done, 1)

                    def add(p, s, e, scale, step):
                        if step > 2:
                            hold(dve, x1_done, 4 * p + step - 2)
                        v.scalar_tensor_tensor(rows(p, e), couples(ps_m[s]), scale, rows(p, e),
                                               ALU.mult, ALU.add).then_inc(x1_done, 1)

                    def indices():
                        if f"idx{h}" not in on:
                            return
                        hold(dve, place_done, TILES * (w + 1))
                        if not (isinstance(t, int) and w < 2):
                            hold(dve, idx_saved, 16 * (w - 1))
                        v.tensor_copy(idx16[1 - h][:, :], place[1 - h][:, :, 0]).then_inc(idx_done, 1)

                    def compare():
                        if f"out{h}" not in on:
                            return
                        y = w - 1
                        hold(dve, row_done, 16 * (y + 1))
                        if not (isinstance(t, int) and y < 1):
                            hold(dve, code_done, y)
                        for b in range(BLOCKS):
                            last = v.tensor_scalar(onehot[:, b, :], idx_row[h][:, :],
                                                   cst[:, C_CODE + b:C_CODE + b + 1], None,
                                                   ALU.is_equal)
                        last.then_inc(onehot_done, 1)

                    top(0)
                    early = "no_conv" in on or (first is not None and h == 0)
                    if first is not None and h == 0:
                        gn_part((1, first), "scalars")
                    if f"idx{h}" in on:
                        find(w, TILES - 1, 1 - h)
                    if early:
                        top(1)
                    if early:
                        indices()
                    compare()
                    if not early:
                        indices()
                    if gn is not None and gn[0] == 2 and h == 1:
                        gn_part(gn, "variance")
                    if h == gn_half(gn):
                        gn_part(gn, "means")
                    if not early:
                        top(1)
                    if "vq" in on:
                        find(c, 0, h)
                    if "end" in on and h == 0:
                        hold(dve, seg_done, SEGS * t)
                        add(t - 1, 3, 1, neg_conv_scale, 4)
                    if "no_vq" in on and h == 0:
                        if "convz" in on:
                            lo(dve, t, 0)
                        if "conv" in on:
                            for e in range(2):
                                add_m1(dve, t, e)
                        if "convz" in on:
                            lo(dve, t, 1)
                    if gn is not None and gn[0] == 2 and h == 1:
                        gn_part(gn, "scalars")
                    if "conv" in on and h == 1:
                        hold(dve, seg_done, SEGS * t + 2)
                        hold(dve, xm_done, 2 * (t + 1))
                        add(t, 1, 0, conv_scale, 1)
                        add(t, 1, 1, neg_conv_scale, 2)
                    top(2)
                    if "vq" in on:
                        find(c, 1, h)
                    if h == gn_half(gn):
                        gn_part(gn, "distance")
                    top(3)
                    if "vq" in on:
                        find(c, 2, h)
                    if f"out{h}" in on and "no_conv" not in on:
                        hold(dve, code_done, w)
                        out_pixels = slot(t - L_OUT, h).rearrange("p (r w) -> p r w", w=P)
                        v.scalar_tensor_tensor(out_pixels, code_pixels, code_scale, out_pixels,
                                               ALU.mult, ALU.add).then_inc(out_done, 1)
                    if "conv" in on and h == 1:
                        hold(dve, seg_done, SEGS * t + 3)
                        add(t, 2, 0, conv_scale, 3)
                    if "no_vq" in on and "convz" in on and h == 1:
                        lo(dve, t, 2)
                        lo(dve, t, 3)
                if gn is not None and gn[0] == 1:
                    gn_part(gn, "variance")

            walk(dve, pair)


SU_EMAX = 3
SU_SPLIT = 36
SU_DONE = SU_SPLIT + 2 * (SEGS * KW + BLOCKS) + 1


def walk_loads(sp, pair, setup_over):
    setup_over()
    with sp.Fori(0, L_VQ) as t:
        pair(t, {"stats1"})
    pair(L_VQ, {"stats1", "idx1"})
    full = {"stats1", "idx0", "idx1", "out0", "out1"}
    pair(L_OUT, full)
    pair(L_OUT + 1, full | {"reuse"})
    with sp.Fori(L_OUT + 2, PAIRS - L_LOAD) as t:
        pair(t, full | {"reuse"})
    with sp.Fori(PAIRS - L_LOAD, PAIRS + L_VQ) as t:
        pair(t, full - {"stats1"})
    pair(PAIRS + L_VQ, {"idx0", "out0", "out1"})


def kernel(x, L0_conv_weight, L1_conv_embedding):
    import concourse.bacc as bacc
    from concourse.bass_utils import run_bass_kernel_spmd

    nc = bacc.Bacc("TRN2", target_bir_lowering=False, num_devices=1)
    arrays, args = {}, []
    for name, a in (("x", x), ("weight", L0_conv_weight), ("embedding", L1_conv_embedding),
                    ("const", constants())):
        a = np.ascontiguousarray(a)
        arrays[f"in_{name}"] = a
        args.append(nc.dram_tensor(f"in_{name}", a.shape, mybir.dt.from_np(a.dtype),
                                   kind="ExternalInput").ap())
    args.append(nc.dram_tensor("out_0", x.shape, F32, kind="ExternalOutput").ap())
    args.append(nc.dram_tensor("idx_line", (CH,), F16, kind="Internal").ap())
    program(nc, *args)
    r = run_bass_kernel_spmd(nc, [arrays], core_ids=[0])
    return r.results[0]["out_0"]
```
